# Optimizing a Trainium2 kernel written in Bass

```python
import numpy as np
import jax
import jax.numpy as jnp

def _softmax(x, axis=-1):
    return jax.nn.softmax(x, axis=axis)

def _gelu(x):
    return jax.nn.gelu(x, approximate=True)

def _silu(x):
    return jax.nn.silu(x)

def _sigmoid(x):
    return jax.nn.sigmoid(x)

def _layernorm(x, axis=-1, eps=1e-05):
    m = jnp.mean(x, axis=axis, keepdims=True)
    v = jnp.var(x, axis=axis, keepdims=True)
    return (x - m) / jnp.sqrt(v + eps)

def _scatter_add(tgt, idx, src, axis=0):
    return tgt.at[idx].add(src)

def _segment_sum(src, seg, n):
    return jax.ops.segment_sum(src, seg, n)
kernel_name = 'mk_hybrid_d2_jaxref_r8_728a81'

def setup_inputs(seed: int=0):
    np.random.seed(seed)
    _w = jnp.asarray

    def _L0_attn_a_setup():
        import jax, jax.numpy as jnp
        import numpy as np
        EMBED = 128
        HEADS = 16
        HEAD_DIM = EMBED // HEADS
        RANK = 8
        ALPHA = 16
        SCALING = ALPHA / RANK

        def _lora_linear(x, W, b, A, Bm):
            return x @ W + b + x @ A @ Bm * SCALING
        key = jax.random.key(seed)
        ks = jax.random.split(key, 9)
        s = 0.02
        x = jax.random.normal(ks[0], (4, 256, EMBED), dtype=jnp.float32)
        W_qkv = jax.random.normal(ks[1], (EMBED, 3 * EMBED), dtype=jnp.float32) * s
        b_qkv = jax.random.normal(ks[2], (3 * EMBED,), dtype=jnp.float32) * s
        A_qkv = jax.random.normal(ks[3], (EMBED, RANK), dtype=jnp.float32) * s
        B_qkv = jax.random.normal(ks[4], (RANK, 3 * EMBED), dtype=jnp.float32) * s
        W_proj = jax.random.normal(ks[5], (EMBED, EMBED), dtype=jnp.float32) * s
        b_proj = jax.random.normal(ks[6], (EMBED,), dtype=jnp.float32) * s
        A_proj = jax.random.normal(ks[7], (EMBED, RANK), dtype=jnp.float32) * s
        B_proj = jax.random.normal(ks[8], (RANK, EMBED), dtype=jnp.float32) * s
        return dict(x=x, W_qkv=W_qkv, b_qkv=b_qkv, A_qkv=A_qkv, B_qkv=B_qkv, W_proj=W_proj, b_proj=b_proj, A_proj=A_proj, B_proj=B_proj)
    _L0_attn_a_in = _L0_attn_a_setup()

    def _L0_attn_b_setup():
        import jax, jax.numpy as jnp
        import numpy as np
        N_EMBD = 128
        N_HEAD = 16
        SEQ = 256
        BATCH = 2
        NEG = -1000000000.0
        key = jax.random.key(seed)
        k0, k1, k2 = jax.random.split(key, 3)
        return {'hidden_states': jax.random.normal(k0, (BATCH, SEQ, N_EMBD), dtype=jnp.float32), 'w_attn': jax.random.normal(k1, (3 * N_EMBD, N_EMBD), dtype=jnp.float32) * 0.02, 'b_attn': jnp.zeros((3 * N_EMBD,), dtype=jnp.float32), 'w_proj': jax.random.normal(k2, (N_EMBD, N_EMBD), dtype=jnp.float32) * 0.02, 'b_proj': jnp.zeros((N_EMBD,), dtype=jnp.float32)}
    _L0_attn_b_in = _L0_attn_b_setup()

    def _L0_ffn_setup():
        import jax, jax.numpy as jnp
        import numpy as np
        DIM = 128

        def _reference_tuple_inner(x, W_r, W_k, W_v, mu_r, mu_k):
            B, T, C = x.shape
            x_prev = jnp.concatenate([jnp.zeros((B, 1, C), x.dtype), x[:, :-1, :]], axis=1)
            xr = mu_r * x + (1.0 - mu_r) * x_prev
            xk = mu_k * x + (1.0 - mu_k) * x_prev
            r = jax.nn.sigmoid(jnp.einsum('btc,dc->btd', xr, W_r))
            k = jnp.einsum('btc,dc->btd', xk, W_k)
            k_act = jnp.square(jax.nn.relu(k))
            out = r * jnp.einsum('btc,dc->btd', k_act, W_v)
            new_state = x[:, -1, :]
            return (out, new_state)
        key = jax.random.key(seed)
        ks = jax.random.split(key, 6)
        B, T, C = (8, 256, DIM)
        x = jax.random.normal(ks[0], (B, T, C), dtype=jnp.float32)
        s = 1.0 / np.sqrt(C)
        W_r = jax.random.uniform(ks[1], (C, C), jnp.float32, -s, s)
        W_k = jax.random.uniform(ks[2], (C, C), jnp.float32, -s, s)
        W_v = jax.random.uniform(ks[3], (C, C), jnp.float32, -s, s)
        mu_r = jax.random.uniform(ks[4], (C,), jnp.float32)
        mu_k = jax.random.uniform(ks[5], (C,), jnp.float32)
        return {'x': x, 'W_r': W_r, 'W_k': W_k, 'W_v': W_v, 'mu_r': mu_r, 'mu_k': mu_k}
    _L0_ffn_in = _L0_ffn_setup()

    def _L1_attn_a_setup():
        import jax, jax.numpy as jnp
        import numpy as np
        DIM, HID, K, B, S = (128, 192, 4, 4, 512)
        EPS = 1e-05
        C = 8.0

        def rmsnorm(x, w):
            return x * jax.lax.rsqrt(jnp.mean(x * x, axis=-1, keepdims=True) + EPS) * w

        def _rg_lru(u, rg_in_w, rg_in_b, rg_gate_w, rg_gate_b, forget_lambda):
            ig = jnp.einsum('bsh,gh->bsg', u, rg_in_w) + rg_in_b
            rg = jnp.einsum('bsh,gh->bsg', u, rg_gate_w) + rg_gate_b
            alpha = jnp.exp(-C * jax.nn.softplus(forget_lambda) * jax.nn.sigmoid(rg))
            beta = jnp.sqrt(1.0 - alpha * alpha + 1e-06)
            xbeta = beta * jax.nn.sigmoid(ig) * u

            def combine(e1, e2):
                a1, b1 = e1
                a2, b2 = e2
                return (a2 * a1, a2 * b1 + b2)
            _, h = jax.lax.associative_scan(combine, (alpha, xbeta), axis=1)
            return h
        key = jax.random.key(seed)
        ks = jax.random.split(key, 16)
        n = jax.random.normal
        return {'x': n(ks[0], (B, S, DIM), jnp.float32), 'W_in': n(ks[1], (HID, DIM), jnp.float32) * DIM ** (-0.5), 'W_gate': n(ks[2], (HID, DIM), jnp.float32) * DIM ** (-0.5), 'conv_w': n(ks[3], (HID, 1, K), jnp.float32) * (1.0 / K) ** 0.5, 'conv_b': n(ks[4], (HID,), jnp.float32) * 0.02, 'W_out': n(ks[5], (DIM, HID), jnp.float32) * HID ** (-0.5), 'rg_in_w': n(ks[6], (HID, HID), jnp.float32) * HID ** (-0.5), 'rg_in_b': jnp.zeros((HID,), jnp.float32), 'rg_gate_w': n(ks[7], (HID, HID), jnp.float32) * HID ** (-0.5), 'rg_gate_b': jnp.zeros((HID,), jnp.float32), 'forget_lambda': jnp.linspace(-4.323, -9.0, HID, dtype=jnp.float32), 'mlp_gate_w': n(ks[8], (HID, DIM), jnp.float32) * DIM ** (-0.5), 'mlp_up_w': n(ks[9], (HID, DIM), jnp.float32) * DIM ** (-0.5), 'mlp_down_w': n(ks[10], (DIM, HID), jnp.float32) * HID ** (-0.5), 'norm1_w': jnp.ones((DIM,), jnp.float32), 'norm2_w': jnp.ones((DIM,), jnp.float32)}
    _L1_attn_a_in = _L1_attn_a_setup()

    def _L1_attn_b_setup():
        import jax, jax.numpy as jnp
        import numpy as np
        D_MODEL = 128
        N_HEAD = 16
        HEAD_DIM = D_MODEL // N_HEAD
        key = jax.random.key(seed)
        ks = jax.random.split(key, 9)
        s = 1.0 / np.sqrt(D_MODEL)
        x = jax.random.normal(ks[0], (4, 256, D_MODEL), dtype=jnp.float32)
        Wq = jax.random.uniform(ks[1], (D_MODEL, D_MODEL), jnp.float32, -s, s)
        bq = jax.random.uniform(ks[2], (D_MODEL,), jnp.float32, -s, s)
        Wk = jax.random.uniform(ks[3], (D_MODEL, D_MODEL), jnp.float32, -s, s)
        bk = jax.random.uniform(ks[4], (D_MODEL,), jnp.float32, -s, s)
        Wv = jax.random.uniform(ks[5], (D_MODEL, D_MODEL), jnp.float32, -s, s)
        bv = jax.random.uniform(ks[6], (D_MODEL,), jnp.float32, -s, s)
        Wo = jax.random.uniform(ks[7], (D_MODEL, D_MODEL), jnp.float32, -s, s)
        bo = jax.random.uniform(ks[8], (D_MODEL,), jnp.float32, -s, s)
        return {'x': x, 'Wq': Wq, 'bq': bq, 'Wk': Wk, 'bk': bk, 'Wv': Wv, 'bv': bv, 'Wo': Wo, 'bo': bo}
    _L1_attn_b_in = _L1_attn_b_setup()

    def _L1_ffn_setup():
        import jax, jax.numpy as jnp
        import numpy as np
        DIM = 128
        DEPTH = 6
        HEADS = 16
        DIM_HEAD = 64
        WINDOW = 32
        INNER = HEADS * DIM_HEAD
        DIM_INNER = int(DIM * 4 * 2 / 3)
        QK_SCALE = 8.0

        def shift_tokens(t):
            a, s = jnp.split(t, 2, -1)
            s = jnp.pad(s, ((0, 0), (1, 0), (0, 0)))[:, :-1]
            return jnp.concatenate([a, s], -1)

        def l2norm(t):
            return t / jnp.maximum(jnp.linalg.norm(t, axis=-1, keepdims=True), 1e-12)

        def rotate_half(x):
            x1, x2 = jnp.split(x, 2, -1)
            return jnp.concatenate([-x2, x1], -1)

        def rotary_tables(n):
            half = jnp.arange(0, DIM_HEAD, 2, dtype=jnp.float32)
            inv_freq = 1.0 / 10000.0 ** (half / DIM_HEAD)
            t = jnp.arange(n, dtype=jnp.float32)
            freqs = t[:, None] * inv_freq[None, :]
            freqs = jnp.concatenate([freqs, freqs], -1)
            base_scale = (half + 0.4 * DIM_HEAD) / (1.4 * DIM_HEAD)
            power = (t - n // 2) / (WINDOW // 2)
            scale = base_scale[None, :] ** power[:, None]
            scale = jnp.concatenate([scale, scale], -1)
            return (freqs, scale)

        def local_attention(q, k, v):
            b, h, n, d = q.shape
            w = WINDOW
            nw = n // w
            bq = q.reshape(b, h, nw, w, d)
            bk = k.reshape(b, h, nw, w, d)
            bv = v.reshape(b, h, nw, w, d)

            def look(t):
                p = jnp.pad(t, ((0, 0), (0, 0), (1, 0), (0, 0), (0, 0)))
                return jnp.concatenate([p[:, :, :nw], p[:, :, 1:]], axis=3)
            bk2, bv2 = (look(bk), look(bv))
            seq = jnp.arange(n).reshape(nw, w)
            seq_p = jnp.pad(seq, ((1, 0), (0, 0)), constant_values=-1)
            jt = jnp.concatenate([seq_p[:nw], seq_p[1:]], axis=1)
            it = seq[:, :, None]
            jb = jt[:, None, :]
            mask = (it < jb) | (it > jb + w) | (jb == -1)
            sim = jnp.einsum('bhwie,bhwje->bhwij', bq, bk2) * QK_SCALE
            sim = jnp.where(mask, -jnp.finfo(sim.dtype).max, sim)
            attn = jax.nn.softmax(sim, -1)
            out = jnp.einsum('bhwij,bhwje->bhwie', attn, bv2)
            return out.reshape(b, h, n, d)

        def attn_layer(x, Wqkv, qs, ksc, Wo):
            b, n, _ = x.shape
            qkv = x @ Wqkv
            q, k, v = jnp.split(qkv, 3, -1)
            sh = lambda t: t.reshape(b, n, HEADS, DIM_HEAD).transpose(0, 2, 1, 3)
            q, k, v = (sh(q), sh(k), sh(v))
            q = l2norm(q) * qs
            k = l2norm(k) * ksc
            freqs, scale = rotary_tables(n)
            cos, sin = (jnp.cos(freqs), jnp.sin(freqs))
            q = q * cos * scale + rotate_half(q) * sin * scale
            inv = 1.0 / scale
            k = k * cos * inv + rotate_half(k) * sin * inv
            out = local_attention(q, k, v)
            out = out.transpose(0, 2, 1, 3).reshape(b, n, INNER)
            return out @ Wo

        def ffn_layer(x, g, bln, W1, b1, W2, b2):
            mu = x.mean(-1, keepdims=True)
            var = ((x - mu) ** 2).mean(-1, keepdims=True)
            xn = (x - mu) / jnp.sqrt(var + 1e-05) * g + bln
            hg = xn @ W1 + b1
            a, gate = jnp.split(hg, 2, -1)
            return a * jax.nn.gelu(gate, approximate=False) @ W2 + b2
        key = jax.random.key(seed)
        ks = jax.random.split(key, 8)
        B, N = (2, 256)
        init = lambda k, shape: jax.random.normal(k, shape, jnp.float32) * 0.02
        return {'x': jax.random.normal(ks[0], (B, N, DIM), jnp.float32), 'Wqkv': init(ks[1], (DEPTH, DIM, 3 * INNER)), 'q_scale': jnp.ones((DEPTH, DIM_HEAD), jnp.float32), 'k_scale': jnp.ones((DEPTH, DIM_HEAD), jnp.float32), 'Wo': init(ks[2], (DEPTH, INNER, DIM)), 'ln_g': jnp.ones((DEPTH, DIM), jnp.float32), 'ln_b': jnp.zeros((DEPTH, DIM), jnp.float32), 'W1': init(ks[3], (DEPTH, DIM, 2 * DIM_INNER)), 'b1': jnp.zeros((DEPTH, 2 * DIM_INNER), jnp.float32), 'W2': init(ks[4], (DEPTH, DIM_INNER, DIM)), 'b2': jnp.zeros((DEPTH, DIM), jnp.float32)}
    _L1_ffn_in = _L1_ffn_setup()
    _d = {'L0_attn_a_x': _L0_attn_a_in['x'], 'L0_attn_a_W_qkv': _L0_attn_a_in['W_qkv'], 'L0_attn_a_b_qkv': _L0_attn_a_in['b_qkv'], 'L0_attn_a_A_qkv': _L0_attn_a_in['A_qkv'], 'L0_attn_a_B_qkv': _L0_attn_a_in['B_qkv'], 'L0_attn_a_W_proj': _L0_attn_a_in['W_proj'], 'L0_attn_a_b_proj': _L0_attn_a_in['b_proj'], 'L0_attn_a_A_proj': _L0_attn_a_in['A_proj'], 'L0_attn_a_B_proj': _L0_attn_a_in['B_proj'], 'L0_attn_b_w_attn': _L0_attn_b_in['w_attn'], 'L0_attn_b_b_attn': _L0_attn_b_in['b_attn'], 'L0_attn_b_w_proj': _L0_attn_b_in['w_proj'], 'L0_attn_b_b_proj': _L0_attn_b_in['b_proj'], 'L0_ffn_W_r': _L0_ffn_in['W_r'], 'L0_ffn_W_k': _L0_ffn_in['W_k'], 'L0_ffn_W_v': _L0_ffn_in['W_v'], 'L0_ffn_mu_r': _L0_ffn_in['mu_r'], 'L0_ffn_mu_k': _L0_ffn_in['mu_k'], 'L1_attn_a_W_in': _L1_attn_a_in['W_in'], 'L1_attn_a_W_gate': _L1_attn_a_in['W_gate'], 'L1_attn_a_conv_w': _L1_attn_a_in['conv_w'], 'L1_attn_a_conv_b': _L1_attn_a_in['conv_b'], 'L1_attn_a_W_out': _L1_attn_a_in['W_out'], 'L1_attn_a_rg_in_w': _L1_attn_a_in['rg_in_w'], 'L1_attn_a_rg_in_b': _L1_attn_a_in['rg_in_b'], 'L1_attn_a_rg_gate_w': _L1_attn_a_in['rg_gate_w'], 'L1_attn_a_rg_gate_b': _L1_attn_a_in['rg_gate_b'], 'L1_attn_a_forget_lambda': _L1_attn_a_in['forget_lambda'], 'L1_attn_a_mlp_gate_w': _L1_attn_a_in['mlp_gate_w'], 'L1_attn_a_mlp_up_w': _L1_attn_a_in['mlp_up_w'], 'L1_attn_a_mlp_down_w': _L1_attn_a_in['mlp_down_w'], 'L1_attn_a_norm1_w': _L1_attn_a_in['norm1_w'], 'L1_attn_a_norm2_w': _L1_attn_a_in['norm2_w'], 'L1_attn_b_Wq': _L1_attn_b_in['Wq'], 'L1_attn_b_bq': _L1_attn_b_in['bq'], 'L1_attn_b_Wk': _L1_attn_b_in['Wk'], 'L1_attn_b_bk': _L1_attn_b_in['bk'], 'L1_attn_b_Wv': _L1_attn_b_in['Wv'], 'L1_attn_b_bv': _L1_attn_b_in['bv'], 'L1_attn_b_Wo': _L1_attn_b_in['Wo'], 'L1_attn_b_bo': _L1_attn_b_in['bo'], 'L1_ffn_Wqkv': _L1_ffn_in['Wqkv'], 'L1_ffn_q_scale': _L1_ffn_in['q_scale'], 'L1_ffn_k_scale': _L1_ffn_in['k_scale'], 'L1_ffn_Wo': _L1_ffn_in['Wo'], 'L1_ffn_ln_g': _L1_ffn_in['ln_g'], 'L1_ffn_ln_b': _L1_ffn_in['ln_b'], 'L1_ffn_W1': _L1_ffn_in['W1'], 'L1_ffn_b1': _L1_ffn_in['b1'], 'L1_ffn_W2': _L1_ffn_in['W2'], 'L1_ffn_b2': _L1_ffn_in['b2']}
    _x0 = _d['L0_attn_a_x']
    _d['L0_attn_a_x'] = jax.random.normal(jax.random.fold_in(jax.random.key(seed), 1), (2, 1024, 128), dtype=_x0.dtype)
    del _x0
    return _d

def reference(L0_attn_a_x, L0_attn_a_W_qkv, L0_attn_a_b_qkv, L0_attn_a_A_qkv, L0_attn_a_B_qkv, L0_attn_a_W_proj, L0_attn_a_b_proj, L0_attn_a_A_proj, L0_attn_a_B_proj, L0_attn_b_w_attn, L0_attn_b_b_attn, L0_attn_b_w_proj, L0_attn_b_b_proj, L0_ffn_W_r, L0_ffn_W_k, L0_ffn_W_v, L0_ffn_mu_r, L0_ffn_mu_k, L1_attn_a_W_in, L1_attn_a_W_gate, L1_attn_a_conv_w, L1_attn_a_conv_b, L1_attn_a_W_out, L1_attn_a_rg_in_w, L1_attn_a_rg_in_b, L1_attn_a_rg_gate_w, L1_attn_a_rg_gate_b, L1_attn_a_forget_lambda, L1_attn_a_mlp_gate_w, L1_attn_a_mlp_up_w, L1_attn_a_mlp_down_w, L1_attn_a_norm1_w, L1_attn_a_norm2_w, L1_attn_b_Wq, L1_attn_b_bq, L1_attn_b_Wk, L1_attn_b_bk, L1_attn_b_Wv, L1_attn_b_bv, L1_attn_b_Wo, L1_attn_b_bo, L1_ffn_Wqkv, L1_ffn_q_scale, L1_ffn_k_scale, L1_ffn_Wo, L1_ffn_ln_g, L1_ffn_ln_b, L1_ffn_W1, L1_ffn_b1, L1_ffn_W2, L1_ffn_b2):

    def _L0_attn_a_ref(x, W_qkv, b_qkv, A_qkv, B_qkv, W_proj, b_proj, A_proj, B_proj):
        import jax, jax.numpy as jnp
        import numpy as np
        EMBED = 128
        HEADS = 16
        HEAD_DIM = EMBED // HEADS
        RANK = 8
        ALPHA = 16
        SCALING = ALPHA / RANK

        def _lora_linear(x, W, b, A, Bm):
            return x @ W + b + x @ A @ Bm * SCALING
        B, N, C = x.shape
        qkv = _lora_linear(x, W_qkv, b_qkv, A_qkv, B_qkv)
        qkv = qkv.reshape(B, N, 3, HEADS, HEAD_DIM).transpose(2, 0, 3, 1, 4)
        q, k, v = (qkv[0], qkv[1], qkv[2])
        attn = jnp.einsum('bhnd,bhmd->bhnm', q, k) * HEAD_DIM ** (-0.5)
        attn = jax.nn.softmax(attn, axis=-1)
        out = jnp.einsum('bhnm,bhmd->bhnd', attn, v)
        out = out.transpose(0, 2, 1, 3).reshape(B, N, C)
        return _lora_linear(out, W_proj, b_proj, A_proj, B_proj)

    def _L0_attn_b_ref(hidden_states, w_attn, b_attn, w_proj, b_proj):
        import jax, jax.numpy as jnp
        import numpy as np
        N_EMBD = 128
        N_HEAD = 16
        SEQ = 256
        BATCH = 2
        NEG = -1000000000.0
        B, S, E = hidden_states.shape
        H = N_HEAD
        D = E // H
        qkv = hidden_states @ w_attn.T + b_attn
        q, k, v = jnp.split(qkv, 3, axis=-1)
        split = lambda t: t.reshape(B, S, H, D).transpose(0, 2, 1, 3)
        q, k, v = (split(q), split(k), split(v))
        w = jnp.einsum('bhnd,bhmd->bhnm', q, k) * jax.lax.rsqrt(float(D))
        mask = jnp.tril(jnp.ones((S, S), dtype=jnp.float32))
        w = jnp.where(mask > 0, w, NEG)
        w = jax.nn.softmax(w, axis=-1)
        attn = jnp.einsum('bhnm,bhmd->bhnd', w, v)
        attn = attn.transpose(0, 2, 1, 3).reshape(B, S, E)
        return attn @ w_proj.T + b_proj

    def _L0_ffn_ref(x, W_r, W_k, W_v, mu_r, mu_k):
        import jax, jax.numpy as jnp
        import numpy as np
        DIM = 128

        def _reference_tuple_inner(x, W_r, W_k, W_v, mu_r, mu_k):
            B, T, C = x.shape
            x_prev = jnp.concatenate([jnp.zeros((B, 1, C), x.dtype), x[:, :-1, :]], axis=1)
            xr = mu_r * x + (1.0 - mu_r) * x_prev
            xk = mu_k * x + (1.0 - mu_k) * x_prev
            r = jax.nn.sigmoid(jnp.einsum('btc,dc->btd', xr, W_r))
            k = jnp.einsum('btc,dc->btd', xk, W_k)
            k_act = jnp.square(jax.nn.relu(k))
            out = r * jnp.einsum('btc,dc->btd', k_act, W_v)
            new_state = x[:, -1, :]
            return (out, new_state)
        return _reference_tuple_inner(x, W_r, W_k, W_v, mu_r, mu_k)[0]

    def _L1_attn_a_ref(x, W_in, W_gate, conv_w, conv_b, W_out, rg_in_w, rg_in_b, rg_gate_w, rg_gate_b, forget_lambda, mlp_gate_w, mlp_up_w, mlp_down_w, norm1_w, norm2_w):
        import jax, jax.numpy as jnp
        import numpy as np
        DIM, HID, K, B, S = (128, 192, 4, 4, 512)
        EPS = 1e-05
        C = 8.0

        def rmsnorm(x, w):
            return x * jax.lax.rsqrt(jnp.mean(x * x, axis=-1, keepdims=True) + EPS) * w

        def _rg_lru(u, rg_in_w, rg_in_b, rg_gate_w, rg_gate_b, forget_lambda):
            ig = jnp.einsum('bsh,gh->bsg', u, rg_in_w) + rg_in_b
            rg = jnp.einsum('bsh,gh->bsg', u, rg_gate_w) + rg_gate_b
            alpha = jnp.exp(-C * jax.nn.softplus(forget_lambda) * jax.nn.sigmoid(rg))
            beta = jnp.sqrt(1.0 - alpha * alpha + 1e-06)
            xbeta = beta * jax.nn.sigmoid(ig) * u

            def combine(e1, e2):
                a1, b1 = e1
                a2, b2 = e2
                return (a2 * a1, a2 * b1 + b2)
            _, h = jax.lax.associative_scan(combine, (alpha, xbeta), axis=1)
            return h
        seq_len = x.shape[1]
        h = rmsnorm(x, norm1_w)
        gate = jnp.einsum('bsd,hd->bsh', h, W_gate)
        u = jnp.einsum('bsd,hd->bsh', h, W_in)
        uc = jax.lax.conv_general_dilated(u.transpose(0, 2, 1), conv_w, window_strides=(1,), padding=[(K - 1, 0)], dimension_numbers=('NCH', 'OIH', 'NCH'), feature_group_count=HID)
        u = (uc + conv_b[None, :, None]).transpose(0, 2, 1)[:, :seq_len, :]
        hrec = _rg_lru(u, rg_in_w, rg_in_b, rg_gate_w, rg_gate_b, forget_lambda)
        mix = jnp.einsum('bsh,dh->bsd', jax.nn.gelu(gate, approximate=False) * hrec, W_out)
        x = x + mix
        n2 = rmsnorm(x, norm2_w)
        g = jax.nn.gelu(jnp.einsum('bsd,hd->bsh', n2, mlp_gate_w), approximate=False)
        up = jnp.einsum('bsd,hd->bsh', n2, mlp_up_w)
        mlp = jnp.einsum('bsh,dh->bsd', g * up, mlp_down_w)
        return x + mlp

    def _L1_attn_b_ref(x, Wq, bq, Wk, bk, Wv, bv, Wo, bo):
        import jax, jax.numpy as jnp
        import numpy as np
        D_MODEL = 128
        N_HEAD = 16
        HEAD_DIM = D_MODEL // N_HEAD
        B, S, _ = x.shape
        scale = jnp.sqrt(jnp.float32(HEAD_DIM))

        def split_heads(t):
            return t.reshape(B, S, N_HEAD, HEAD_DIM).transpose(0, 2, 1, 3)
        Q = split_heads(x @ Wq.T + bq)
        K = split_heads(x @ Wk.T + bk)
        V = split_heads(x @ Wv.T + bv)
        scores = jnp.einsum('bhqd,bhkd->bhqk', Q, K) / scale
        attn = jax.nn.softmax(scores, axis=-1)
        out = jnp.einsum('bhqk,bhkd->bhqd', attn, V)
        out = out.transpose(0, 2, 1, 3).reshape(B, S, D_MODEL)
        return out @ Wo.T + bo

    def _L1_ffn_ref(x, Wqkv, q_scale, k_scale, Wo, ln_g, ln_b, W1, b1, W2, b2):
        import jax, jax.numpy as jnp
        import numpy as np
        DIM = 128
        DEPTH = 6
        HEADS = 16
        DIM_HEAD = 64
        WINDOW = 32
        INNER = HEADS * DIM_HEAD
        DIM_INNER = int(DIM * 4 * 2 / 3)
        QK_SCALE = 8.0

        def shift_tokens(t):
            a, s = jnp.split(t, 2, -1)
            s = jnp.pad(s, ((0, 0), (1, 0), (0, 0)))[:, :-1]
            return jnp.concatenate([a, s], -1)

        def l2norm(t):
            return t / jnp.maximum(jnp.linalg.norm(t, axis=-1, keepdims=True), 1e-12)

        def rotate_half(x):
            x1, x2 = jnp.split(x, 2, -1)
            return jnp.concatenate([-x2, x1], -1)

        def rotary_tables(n):
            half = jnp.arange(0, DIM_HEAD, 2, dtype=jnp.float32)
            inv_freq = 1.0 / 10000.0 ** (half / DIM_HEAD)
            t = jnp.arange(n, dtype=jnp.float32)
            freqs = t[:, None] * inv_freq[None, :]
            freqs = jnp.concatenate([freqs, freqs], -1)
            base_scale = (half + 0.4 * DIM_HEAD) / (1.4 * DIM_HEAD)
            power = (t - n // 2) / (WINDOW // 2)
            scale = base_scale[None, :] ** power[:, None]
            scale = jnp.concatenate([scale, scale], -1)
            return (freqs, scale)

        def local_attention(q, k, v):
            b, h, n, d = q.shape
            w = WINDOW
            nw = n // w
            bq = q.reshape(b, h, nw, w, d)
            bk = k.reshape(b, h, nw, w, d)
            bv = v.reshape(b, h, nw, w, d)

            def look(t):
                p = jnp.pad(t, ((0, 0), (0, 0), (1, 0), (0, 0), (0, 0)))
                return jnp.concatenate([p[:, :, :nw], p[:, :, 1:]], axis=3)
            bk2, bv2 = (look(bk), look(bv))
            seq = jnp.arange(n).reshape(nw, w)
            seq_p = jnp.pad(seq, ((1, 0), (0, 0)), constant_values=-1)
            jt = jnp.concatenate([seq_p[:nw], seq_p[1:]], axis=1)
            it = seq[:, :, None]
            jb = jt[:, None, :]
            mask = (it < jb) | (it > jb + w) | (jb == -1)
            sim = jnp.einsum('bhwie,bhwje->bhwij', bq, bk2) * QK_SCALE
            sim = jnp.where(mask, -jnp.finfo(sim.dtype).max, sim)
            attn = jax.nn.softmax(sim, -1)
            out = jnp.einsum('bhwij,bhwje->bhwie', attn, bv2)
            return out.reshape(b, h, n, d)

        def attn_layer(x, Wqkv, qs, ksc, Wo):
            b, n, _ = x.shape
            qkv = x @ Wqkv
            q, k, v = jnp.split(qkv, 3, -1)
            sh = lambda t: t.reshape(b, n, HEADS, DIM_HEAD).transpose(0, 2, 1, 3)
            q, k, v = (sh(q), sh(k), sh(v))
            q = l2norm(q) * qs
            k = l2norm(k) * ksc
            freqs, scale = rotary_tables(n)
            cos, sin = (jnp.cos(freqs), jnp.sin(freqs))
            q = q * cos * scale + rotate_half(q) * sin * scale
            inv = 1.0 / scale
            k = k * cos * inv + rotate_half(k) * sin * inv
            out = local_attention(q, k, v)
            out = out.transpose(0, 2, 1, 3).reshape(b, n, INNER)
            return out @ Wo

        def ffn_layer(x, g, bln, W1, b1, W2, b2):
            mu = x.mean(-1, keepdims=True)
            var = ((x - mu) ** 2).mean(-1, keepdims=True)
            xn = (x - mu) / jnp.sqrt(var + 1e-05) * g + bln
            hg = xn @ W1 + b1
            a, gate = jnp.split(hg, 2, -1)
            return a * jax.nn.gelu(gate, approximate=False) @ W2 + b2
        for i in range(DEPTH):
            x = attn_layer(shift_tokens(x), Wqkv[i], q_scale[i], k_scale[i], Wo[i]) + x
            x = ffn_layer(shift_tokens(x), ln_g[i], ln_b[i], W1[i], b1[i], W2[i], b2[i]) + x
        return x
    x = L0_attn_a_x
    x = x + _L0_attn_a_ref(_layernorm(x, axis=-1), L0_attn_a_W_qkv, L0_attn_a_b_qkv, L0_attn_a_A_qkv, L0_attn_a_B_qkv, L0_attn_a_W_proj, L0_attn_a_b_proj, L0_attn_a_A_proj, L0_attn_a_B_proj)
    x = x + _L0_ffn_ref(_layernorm(x, axis=-1), L0_ffn_W_r, L0_ffn_W_k, L0_ffn_W_v, L0_ffn_mu_r, L0_ffn_mu_k)
    x = x + _L0_attn_b_ref(_layernorm(x, axis=-1), L0_attn_b_w_attn, L0_attn_b_b_attn, L0_attn_b_w_proj, L0_attn_b_b_proj)
    x = x + _L0_ffn_ref(_layernorm(x, axis=-1), L0_ffn_W_r, L0_ffn_W_k, L0_ffn_W_v, L0_ffn_mu_r, L0_ffn_mu_k)
    x = x + _L1_attn_a_ref(_layernorm(x, axis=-1), L1_attn_a_W_in, L1_attn_a_W_gate, L1_attn_a_conv_w, L1_attn_a_conv_b, L1_attn_a_W_out, L1_attn_a_rg_in_w, L1_attn_a_rg_in_b, L1_attn_a_rg_gate_w, L1_attn_a_rg_gate_b, L1_attn_a_forget_lambda, L1_attn_a_mlp_gate_w, L1_attn_a_mlp_up_w, L1_attn_a_mlp_down_w, L1_attn_a_norm1_w, L1_attn_a_norm2_w)
    x = x + _L1_ffn_ref(_layernorm(x, axis=-1), L1_ffn_Wqkv, L1_ffn_q_scale, L1_ffn_k_scale, L1_ffn_Wo, L1_ffn_ln_g, L1_ffn_ln_b, L1_ffn_W1, L1_ffn_b1, L1_ffn_W2, L1_ffn_b2)
    x = x + _L1_attn_b_ref(_layernorm(x, axis=-1), L1_attn_b_Wq, L1_attn_b_bq, L1_attn_b_Wk, L1_attn_b_bk, L1_attn_b_Wv, L1_attn_b_bv, L1_attn_b_Wo, L1_attn_b_bo)
    x = x + _L1_ffn_ref(_layernorm(x, axis=-1), L1_ffn_Wqkv, L1_ffn_q_scale, L1_ffn_k_scale, L1_ffn_Wo, L1_ffn_ln_g, L1_ffn_ln_b, L1_ffn_W1, L1_ffn_b1, L1_ffn_W2, L1_ffn_b2)
    return x

_drawn_inputs = setup_inputs


def setup_inputs(seed=0):
    import zlib

    import numpy as np

    out = dict(_drawn_inputs(seed))
    spreads = {'L0_attn_b_b_attn': (0.0, 0.631),
     'L0_attn_b_b_proj': (0.0, 0.1),
     'L1_attn_a_rg_in_b': (0.0, 0.47),
     'L1_attn_a_rg_gate_b': (0.0, 0.8),
     'L1_attn_a_norm1_w': (1.0, 0.2),
     'L1_attn_a_norm2_w': (1.0, 0.2),
     'L1_ffn_q_scale': (1.0, 0.6),
     'L1_ffn_k_scale': (1.0, 0.6),
     'L1_ffn_ln_g': (1.0, 0.6),
     'L1_ffn_ln_b': (0.0, 0.8),
     'L1_ffn_b1': (0.0, 0.8),
     'L1_ffn_b2': (0.0, 0.1)}
    factors = {'L0_attn_a_W_qkv': 8.0,
     'L0_attn_a_b_qkv': 4.418,
     'L0_attn_a_A_qkv': 8.0,
     'L0_attn_a_B_qkv': 8.0,
     'L0_attn_a_W_proj': 3.704,
     'L0_attn_a_A_proj': 8.0,
     'L0_attn_a_B_proj': 8.0,
     'L0_attn_b_w_attn': 5.111,
     'L0_ffn_mu_r': 12.597,
     'L1_attn_b_Wq': 8.0,
     'L1_attn_b_bq': 49.551,
     'L1_attn_b_Wk': 8.0,
     'L1_attn_b_bk': 64.0,
     'L1_attn_b_bv': 17.46,
     'L1_attn_b_bo': 9.973,
     'L1_ffn_W1': 3.375,
     'L1_ffn_W2': 3.323,
     'L0_attn_a_b_proj': 5.315}
    for name, (base, spread) in spreads.items():
        noise = np.random.default_rng([zlib.crc32(name.encode()), seed]).standard_normal(out[name].shape)
        drawn = base * np.exp(spread * noise) if base else spread * noise
        out[name] = jnp.asarray(drawn.astype(out[name].dtype))
    for name, factor in factors.items():
        out[name] = (out[name] * factor).astype(out[name].dtype)
    return out
```

```python
from contextlib import ExitStack, contextmanager

import numpy as np

import concourse.bass as bass
from concourse import mybir

F32, F32R, BF16 = mybir.dt.float32, mybir.dt.float32r, mybir.dt.bfloat16
ACT = mybir.ActivationFunctionType
ALU = mybir.AluOpType
AX = mybir.AxisListType

B, N, C = 2, 1024, 128
TILES = B * N // 128
BT = N // 128
PAD = 32
XW = PAD + N + 32
NEG = -1.0e30
EPS = 1e-5
LN_EXP_SET = 6

HEADS, HD = 16, 8
HGROUPS = B * HEADS // 4
KROWS = 9 * HD

PAIRS = 8
ARENA = 34200
QC = 96
CHUNKS = -(-N // QC)
QW = CHUNKS * QC
DEPTH = 6
INNER = 341

HID = 192


def shape_constants():
    i = np.arange(128)
    out = {"c_ident": np.eye(128, dtype=np.float32)}
    j, q = i[:, None], np.arange(QC)[None, :]
    band = (q + 32 - j >= 0) & (q + 32 - j <= 32)
    first = band & (j >= 32)
    for name, ok in (("c_band", band), ("c_band0", first)):
        out[name + "_kq"] = np.where(ok, 0.0, NEG).astype(np.float32)
        out[name + "_qk"] = np.ascontiguousarray(out[name + "_kq"].T)
    c = np.arange(128)[None, :]
    out["c_causal_kq"] = np.where(c >= i[:, None], 0.0, NEG).astype(np.float32)
    out["c_causal_qk"] = np.where(c <= i[:, None], 0.0, NEG).astype(np.float32)
    d = 64
    half = np.arange(0, d, 2, dtype=np.float32)
    t = np.arange(N, dtype=np.float32)
    freqs = t[:, None] * (np.float32(1.0) / np.float32(10000.0) ** (half / np.float32(d)))[None, :]
    freqs = np.concatenate([freqs, freqs], -1).astype(np.float32)
    base = ((half + np.float32(0.4 * d)) / np.float32(1.4 * d)).astype(np.float32)
    power = ((t - N // 2) / 16).astype(np.float32)
    scale = (base[None, :] ** power[:, None]).astype(np.float32)
    scale = np.concatenate([scale, scale], -1)
    inv = (np.float32(1.0) / scale).astype(np.float32)
    cos, sin = np.cos(freqs), np.sin(freqs)
    sign = np.where(np.arange(d) < d // 2, -1.0, 1.0).astype(np.float32)
    tab_a = np.stack([8 * cos * scale, cos * inv], 1)
    tab_b = np.stack([8 * sin * scale * sign, sin * inv * sign], 1)
    for name, tab in (("c_rot_a", tab_a), ("c_rot_b", tab_b)):
        out[name] = np.ascontiguousarray(tab.reshape(BT, 128, 2, d).transpose(1, 0, 2, 3).reshape(128, -1).astype(np.float32))
    return out


def build(nc, I, out):
    ctx = ExitStack()

    def sb(name, shape, dt=F32):
        return ctx.enter_context(nc.sbuf_tensor(name, shape, dt))

    pool_of_sems = {}

    def sem(name):
        if name not in pool_of_sems:
            pool_of_sems[name] = nc.alloc_semaphore(name)
        return pool_of_sems[name]

    @contextmanager
    def stage(*names):
        sems = [sem(n) for n in names]
        with nc.Block() as block:
            yield (block, *sems)
        numbers = sorted(s.num for s in sems)
        while numbers:
            n = next((n for n in range(1, len(numbers)) if numbers[n] != numbers[0] + n), len(numbers))
            nc.gpsimd.sem_clear(range(numbers[0], numbers[0] + n))
            numbers = numbers[n:]
        nc.all_engine_barrier()

    def linker(eng, s):
        count = [0]

        def link(ins):
            count[0] += 1
            ins.then_inc(s, 1)
            eng.wait_ge(s, count[0])
        return link

    x_tok = sb("x_tok", [128, TILES, C])
    arena = sb("arena", [128, ARENA])
    PS = ctx.enter_context(nc.psum_tensor("PS", [128, 8, 512], F32))

    class Cut:
        at = 0

    def cut(n, at=None):
        if at is not None:
            Cut.at = at
        a = arena[:, Cut.at:Cut.at + n]
        Cut.at += n
        assert Cut.at <= ARENA, Cut.at
        return a

    ident = sb("ident", [128, 128])
    ident_b = sb("ident_b", [128, 128], BF16)
    ones = sb("ones", [128, 128])
    ones_r = sb("ones_r", [128, 128], F32R)
    band_kq = [sb(f"band{m}_kq", [128, QC], BF16) for m in range(2)]
    band_qk = [sb(f"band{m}_qk", [QC, 128], BF16) for m in range(2)]
    causal_kq = sb("causal_kq", [128, 128], BF16)
    causal_qk = sb("causal_qk", [128, 128], BF16)
    consts = sb("consts", [128, 4])
    eps_ap, rms_eps, ln256 = (consts[:, n:n + 1] for n in range(3))
    stats = sb("stats", [128, TILES, 6])
    moments = sb("moments", [128, TILES, 2])
    rstd = sb("rstd", [128, TILES])
    wbuf = sb("wbuf", [128, 2080])

    XT = cut(B * XW, 0).rearrange("p (b n) -> p b n", b=B)
    after_xt = Cut.at

    w1 = sb("w1", [128, 2 * INNER])
    w2 = sb("w2", [128, 3, C])
    ff_cols = sb("ff_cols", [128, 8])
    b2_row = sb("b2_row", [128, C])
    x_keep = sb("x_keep", [128, TILES, C])
    x_parts = [sb(f"x_{name}", [128, B * N], F32R) for name in ("high", "low")]
    w_parts = [sb(f"w_qk_{name}", [128, 256], F32R) for name in ("high", "low")]
    w1_parts = [sb(f"w1_{name}", [128, 2 * INNER], F32R) for name in ("high", "low")]
    PRODUCTS = ((0, 0), (0, 1), (1, 0))
    diag = [sb(f"diag{m}", [128, 4 * QC], F32R) for m in range(3)]

    dram = {}

    def scratch(name, shape, dt):
        if name not in dram:
            dram[name] = nc.dram_tensor(name, shape, dt, kind="Internal").ap()
        return dram[name]

    def tokens(k):
        return XT[:, k // 2, PAD + 512 * (k % 2):PAD + 512 * (k % 2) + 512]

    def setup():
        st = cut(3000, after_xt)
        with stage("loaded", "made") as (block, loaded, made):
            @block.sync
            def _(sp):
                sp.dma_start(x_tok[:, :, :], I["L0_attn_a_x"].rearrange("b (t p) c -> p (b t) c", p=128)).then_inc(loaded, 16)
                sp.dma_start(ident[:, :], I["c_ident"]).then_inc(loaded, 16)
                sp.dma_start(st[:, 0:128], I["c_causal_kq"]).then_inc(loaded, 16)
                sp.dma_start(st[:, 896:1024], I["c_causal_qk"]).then_inc(loaded, 16)
                for m, name in enumerate(("c_band", "c_band0")):
                    sp.dma_start(st[:, 1792 + 96 * m:1888 + 96 * m], I[name + "_kq"]).then_inc(loaded, 16)
                    sp.dma_start(st[0:QC, 2048 + 128 * m:2176 + 128 * m], I[name + "_qk"]).then_inc(loaded, 16)

            @block.gpsimd
            def _(pool):
                nc.gpsimd.memset(XT[:, :, :], 0.0).then_inc(made, 1)
                nc.gpsimd.memset(ones[:, :], 1.0).then_inc(made, 1)
                for n, v in enumerate((EPS, 1e-6, 8.0 * float(np.log(2.0)), 0.0)):
                    nc.gpsimd.memset(consts[:, n:n + 1], v).then_inc(made, 1)
                pool.wait_ge(made, 6)

            @block.vector
            def _(dve):
                dve.wait_ge(loaded, 8 * 16)
                nc.vector.tensor_copy(ident_b[:, :], ident[:, :])
                nc.vector.tensor_copy(causal_kq[:, :], st[:, 0:128])
                nc.vector.tensor_copy(causal_qk[:, :], st[:, 896:1024])
                for m in range(2):
                    nc.vector.tensor_copy(band_kq[m][:, :], st[:, 1792 + 96 * m:1888 + 96 * m])
                    nc.vector.tensor_copy(band_qk[m][:, :], st[0:QC, 2048 + 128 * m:2176 + 128 * m])
                dve.wait_ge(made, 2)
                nc.vector.tensor_copy(ones_r[:, :], ones[:, :])

    def load_ln_exp():
        nc.scalar.add_instruction(mybir.InstLoadActFuncSet(name=nc.get_next_instruction_name(), act_func_set_id=LN_EXP_SET))

    def layernorm_to_xt(loads):
        xn = cut(TILES * C, after_xt).rearrange("p (t c) -> p t c", t=TILES)
        with stage("w_in", "stat", "lnv", "rs", "normed", "turned") as (block, w_in, stat, lnv, rs, normed, turned):
            @block.sync
            def _(sp):
                for dst, src in loads:
                    sp.dma_start(dst, src).then_inc(w_in, 16)
                sp.wait_ge(w_in, 16 * len(loads))

            @block.vector
            def _(dve):
                def moments_of(k):
                    for t in range(4 * k, 4 * k + 4):
                        nc.vector.bn_stats(stats[:, t, :], x_tok[:, t, :]).then_inc(stat, 1)
                    for t in range(4 * k, 4 * k + 4):
                        dve.wait_ge(stat, 8 * k + t % 4 + 1)
                        nc.vector.bn_aggr(moments[:, t, :], stats[:, t, :]).then_inc(stat, 1)

                def normalise(k):
                    dve.wait_ge(rs, k + 1)
                    for t in range(4 * k, 4 * k + 4):
                        nc.vector.tensor_scalar(xn[:, t, :], x_tok[:, t, :], moments[:, t, 0:1], rstd[:, t:t + 1],
                                                ALU.subtract, ALU.mult).then_inc(normed, 1)

                moments_of(0)
                for k in range(1, 4):
                    moments_of(k)
                    normalise(k - 1)
                normalise(3)

            @block.scalar
            def _(act):
                load_ln_exp()

                def rstd_of(k):
                    r = rstd[:, 4 * k:4 * k + 4]
                    act.wait_ge(stat, 8 * k + 8)
                    nc.scalar.activation(r, moments[:, 4 * k:4 * k + 4, 1], ACT.Ln, bias=eps_ap).then_inc(lnv, 1)
                    act.wait_ge(lnv, k + 1)
                    nc.scalar.activation(r, r, ACT.Exp, scale=-0.5).then_inc(rs, 1)

                rstd_of(0)
                rstd_of(1)
                for k in range(4):
                    if k < 2:
                        rstd_of(k + 2)
                    act.wait_ge(turned, 4 * k + 4)
                    nc.scalar.copy(tokens(k), PS[:, k, :])

            @block.tensor
            def _(pe):
                for t in range(TILES):
                    pe.wait_ge(normed, t + 1)
                    nc.tensor.transpose(PS[:, t // 4, 128 * (t % 4):128 * (t % 4) + 128], xn[:, t, :], ident[:, :]).then_inc(turned, 1)

    def channel_mix():
        w_r, w_k, w_v = (wbuf[:, 128 * n:128 * n + 128] for n in range(3))
        mu = wbuf[:, 384:388]
        layernorm_to_xt([(w_r, I["t_W_r"]), (w_k, I["t_W_k"]), (w_v, I["t_W_v"]),
                         (mu[:, 0:1], I["L0_ffn_mu_r"].rearrange("(p o) -> p o", o=1)),
                         (mu[:, 1:2], I["L0_ffn_mu_k"].rearrange("(p o) -> p o", o=1))])
        xr = cut(B * N, after_xt)
        xk = cut(B * N)
        ka = cut(B * N)
        tmp = cut(B * N)
        r_tok = cut(B * N)
        with stage("mixed", "made", "kmm", "kact", "kdone", "rmm", "vmm", "rdone", "vlink") as (
                block, mixed, made, kmm, kact, kdone, rmm, vmm, rdone, vlink):
            @block.vector
            def _(dve):
                nc.vector.tensor_scalar(mu[:, 2:4], mu[:, 0:2], -1.0, 1.0, ALU.mult, ALU.add).then_inc(made, 1)
                dve.wait_ge(made, 1)
                for n, (dst, m) in enumerate(((xk, 1), (xr, 0))):
                    for k in range(4):
                        b, lo = k // 2, PAD + 512 * (k % 2)
                        d = dst[:, 512 * k:512 * k + 512]
                        nc.vector.tensor_scalar(d, XT[:, b, lo - 1:lo + 511], mu[:, 2 + m:3 + m], None, ALU.mult).then_inc(made, 1)
                        dve.wait_ge(made, 2 + 4 * n + k)
                        nc.vector.scalar_tensor_tensor(d, tokens(k), mu[:, m:m + 1], d, ALU.mult, ALU.add).then_inc(mixed, 1)
                for k in range(4):
                    dve.wait_ge(kact, k + 1)
                    d = ka[:, 512 * k:512 * k + 512]
                    nc.vector.tensor_tensor(d, tmp[:, 512 * k:512 * k + 512], tmp[:, 512 * k:512 * k + 512], ALU.mult).then_inc(kdone, 1)
                for k in range(4):
                    dve.wait_ge(rdone, k + 1)
                    dve.wait_ge(vmm, k + 1)
                    r = r_tok[:, 512 * k:512 * k + 512]
                    xs = x_tok[:, 4 * k:4 * k + 4, :]
                    nc.vector.tensor_tensor(r, r, PS[:, 4 + k % 2, :], ALU.mult).then_inc(vlink, 1)
                    dve.wait_ge(vlink, k + 1)
                    nc.vector.tensor_tensor(xs, xs, r.rearrange("p (t c) -> p t c", t=4), ALU.add)

            @block.scalar
            def _(act):
                for k in range(4):
                    act.wait_ge(kmm, k + 1)
                    nc.scalar.activation(tmp[:, 512 * k:512 * k + 512], PS[:, k % 2, :], ACT.Relu).then_inc(kact, 1)
                for k in range(4):
                    act.wait_ge(rmm, k + 1)
                    nc.scalar.activation(r_tok[:, 512 * k:512 * k + 512], PS[:, 2 + k % 2, :], ACT.Sigmoid).then_inc(rdone, 1)

            @block.tensor
            def _(pe):
                for k in range(4):
                    pe.wait_ge(mixed, k + 1)
                    if k >= 2:
                        pe.wait_ge(kact, k - 1)
                    nc.tensor.matmul(PS[:, k % 2, :], w_k, xk[:, 512 * k:512 * k + 512], start=True, stop=True).then_inc(kmm, 1)
                for k in range(4):
                    pe.wait_ge(mixed, 5 + k)
                    if k >= 2:
                        pe.wait_ge(rdone, k - 1)
                    for t in range(4):
                        last = nc.tensor.matmul(PS[:, 2 + k % 2, 128 * t:128 * t + 128], xr[:, 512 * k + 128 * t:512 * k + 128 * t + 128],
                                                w_r, start=True, stop=True)
                    last.then_inc(rmm, 1)
                for k in range(4):
                    pe.wait_ge(kdone, k + 1)
                    if k >= 2:
                        pe.wait_ge(vlink, k - 1)
                    for t in range(4):
                        last = nc.tensor.matmul(PS[:, 4 + k % 2, 128 * t:128 * t + 128], ka[:, 512 * k + 128 * t:512 * k + 128 * t + 128],
                                                w_v, start=True, stop=True)
                    last.then_inc(vmm, 1)


    def full_attention(kind):
        causal = kind == "causal"
        lora = kind == "lora"
        QS = [cut(2 * N, after_xt if m == 0 else None).bitcast(BF16).rearrange("p (h n) -> p h n", h=4) for m in range(2)]
        KS = [cut(2 * N).bitcast(BF16).rearrange("p (h n) -> p h n", h=4) for m in range(2)]
        VB = [cut(BT * 128).rearrange("p (t h d) -> p t h d", t=BT, h=4) for m in range(2)]
        PT = [cut(2 * 512) for m in range(4)]
        OT = [cut(512) for m in range(2)]
        o_tok = cut(HGROUPS * BT * 32).rearrange("p (i t n) -> p i t n", i=HGROUPS, t=BT)
        maxima = cut(64).rearrange("p (h q k) -> p h q k", h=4, q=8)
        neg_max, max_rest = (cut(16).rearrange("p (h q) -> p h q", h=4) for _ in range(2))
        max_parts_flat = cut(16).bitcast(BF16)
        max_parts = max_parts_flat.rearrange("p (h i q) -> p h i q", h=4, i=2)
        max_rows = cut(64).bitcast(BF16)[0:32, :]
        rden = cut(16)
        full_qk = {n: cut(B * N) for n in "qk"}
        rest = {n: cut(N) for n in "qk"}
        parts = {n: cut(3 * B * N // 2).bitcast(BF16).rearrange("p (i n) -> p i n", i=3) for n in "qk"}
        v_all = cut(HGROUPS * BT * 32).rearrange("p (g t e) -> p g t e", g=HGROUPS, t=BT)
        w_qkv, w_p = wbuf[:, 0:384], wbuf[:, 384:512]
        b_qk, b_v, b_p = wbuf[:, 512:514], wbuf[:, 640:768], wbuf[:, 768:896]
        a_qkv_t, b_qkv, a_p_t, b_p_lora = wbuf[0:8, 896:1024], wbuf[0:8, 1024:1408], wbuf[0:8, 1408:1536], wbuf[0:8, 1536:1664]
        scratch_qk = {n: scratch("parts_" + n, [HGROUPS, 3, HD, 4 * N], BF16) for n in "qk"}
        b_q_scaled = wbuf[:, 514:515]

        def row(name, lo, n):
            return I[name][lo:lo + n].rearrange("(o n) -> o n", o=1).broadcast_to([128, n])

        def column(name, lo):
            return I[name][lo:lo + 128].rearrange("(p o) -> p o", o=1)

        if lora:
            loads = [(w_qkv, I["L0_attn_a_W_qkv"]), (w_p, I["L0_attn_a_W_proj"]),
                     (b_qk[:, 0:1], column("L0_attn_a_b_qkv", 0)), (b_qk[:, 1:2], column("L0_attn_a_b_qkv", 128)),
                     (b_v, row("L0_attn_a_b_qkv", 256, 128)), (b_p, row("L0_attn_a_b_proj", 0, 128)),
                     (a_qkv_t, I["t_A_qkv"]), (b_qkv, I["L0_attn_a_B_qkv"]), (a_p_t, I["t_A_proj"]), (b_p_lora, I["L0_attn_a_B_proj"])]
        elif causal:
            loads = [(w_qkv, I["t_w_attn"]), (w_p, I["t_w_proj"]),
                     (b_qk[:, 0:1], column("L0_attn_b_b_attn", 0)), (b_qk[:, 1:2], column("L0_attn_b_b_attn", 128)),
                     (b_v, row("L0_attn_b_b_attn", 256, 128)), (b_p, row("L0_attn_b_b_proj", 0, 128))]
        else:
            loads = [(wbuf[:, 0:128], I["t_Wq"]), (wbuf[:, 128:256], I["t_Wk"]), (wbuf[:, 256:384], I["t_Wv"]), (w_p, I["t_Wo"]),
                     (b_qk[:, 0:1], column("L1_attn_b_bq", 0)), (b_qk[:, 1:2], column("L1_attn_b_bk", 0)),
                     (b_v, row("L1_attn_b_bv", 0, 128)), (b_p, row("L1_attn_b_bo", 0, 128))]

        def keys_of(qt, kh):
            return 128 * (qt % 4) + 128 if causal and kh == qt // 4 else 512

        def first_query(hf, kt):
            return 128 * (kt - 4 * hf) if causal and kt >= 4 * hf else 0

        steps = [(hf, kt) for hf in range(2) for kt in range(8) if not causal or kt < 4 * hf + 4]
        n_steps, n_units = len(steps), 2 * len(steps)
        ends = {hf: max(n for n, s in enumerate(steps) if s[0] == hf) for hf in range(2)}
        max_units = [[(hh, qt, kh) for hh in range(4) for qt in range(4 * hf, 4 * hf + 4) for kh in range(2) if not causal or kh <= qt // 4]
                     for hf in range(2)]
        PER, LEAD = 4, 2 if causal else 3
        n_max = len(max_units[0]) + len(max_units[1])
        own = PER * (ends[0] + 1 - LEAD)
        ahead = len(max_units[1]) - own
        first = len(max_units[0]) + ahead
        assert PER * n_steps == n_max
        LOADS, ROWS = 16 * 6, 16 * 4

        def columns(b):
            return slice(N * b, N * b + N)

        layernorm_to_xt(loads)
        with stage("delta", "weights", "b_scaled", "mm", "evac0", "evac1", "hi", "resid", "mid", "lo", "v_in", "stored0", "stored1",
                   "preset", "vb_ready", "ones_in", "loaded", "rows_in", "st_full", "exp_done", "pv_done", "mx_full", "mx_red", "mlink", "m_ready",
                   "mt_full", "mt_ev", "o_ev", "o_tr", "o_done", "o_done_r", "resid1", "lo1") as (
                block, delta, weights, b_scaled, mm, evac0, evac1, hi, resid, mid, lo, v_in, stored0, stored1,
                preset, vb_ready, ones_in, loaded, rows_in, st_full, exp_done, pv_done, mx_full, mx_red, mlink, m_ready,
                mt_full, mt_ev, o_ev, o_tr, o_done, o_done_r, resid1, lo1):

            def groups(eng, body):
                body(0, 0, False, True)
                with eng.Fori(0, HGROUPS // 2 - 1) as j:
                    body(2 * j + 1, 1, True, True)
                    body(2 * j + 2, 0, True, True)
                body(HGROUPS - 1, 1, True, False)

            def maxima_of_step(i, par, s, has_next):
                for n in range(PER * s, PER * s + PER):
                    if n < own:
                        yield n, par, max_units[1][ahead + n]
                    elif has_next and n < own + len(max_units[0]):
                        yield n, 1 - par, max_units[0][n - own]
                    elif has_next:
                        yield n, 1 - par, max_units[1][n - own - len(max_units[0])]


            @block.sync
            def _(sp):
                def load(i, par):
                    for a in range(3):
                        sp.dma_start(QS[par][24 * a:24 * a + 24, :, :],
                                     scratch_qk["q"][bass.ds(i, 1), a, :, :].broadcast_to([3, HD, 4 * N])).then_inc(loaded, 16)
                        sp.dma_start(KS[par][24 * a:24 * a + 24, :, :],
                                     scratch_qk["k"][bass.ds(i, 1), :, :, :].rearrange("o c d n -> (o c d) n")).then_inc(loaded, 16)

                def rows(half, par, hf):
                    sp.wait_ge(mt_ev, half + 1)
                    for hh in range(4):
                        sp.dma_start(QS[par][KROWS:KROWS + 2, hh, 512 * hf:512 * hf + 512], max_rows[8 * hh:8 * hh + 8, :]).then_inc(rows_in, 16)

                def store(name, part, b, stored):
                    sp.dma_start(scratch_qk[name][4 * b:4 * b + 4, part, :, :].rearrange("g d (h n) -> g (d h) n", h=4),
                                 parts[name][:, part, columns(b)]).then_inc(stored, 16)

                for part, made in enumerate((hi, mid, lo)):
                    for n, name in enumerate("qk"):
                        sp.wait_ge(made, n + 1)
                        store(name, part, 0, stored0)
                sp.wait_ge(ones_in, 4)
                sp.wait_ge(stored0, 6 * 16)
                load(0, 0)
                for n, name in enumerate("qk"):
                    sp.wait_ge(lo1, n + 1)
                    for part in range(3):
                        store(name, part, 1, stored1)
                rows(0, 0, 0)
                sp.wait_ge(stored1, 6 * 16)

                def body(i, par, has_previous, has_next):
                    if has_next:
                        if has_previous:
                            sp.wait_ge(pv_done, i * n_steps)
                        load(i + 1, 1 - par)
                    rows(2 * i + 1, par, 1)
                    if has_next:
                        rows(2 * i + 2, 1 - par, 0)
                groups(sp, body)

            @block.gpsimd
            def _(pool):
                for m in range(2):
                    nc.gpsimd.memset(VB[m], 0.0).then_inc(preset, 1)
                pool.wait_ge(preset, 2)
                for m in range(2):
                    nc.gpsimd.memset(VB[m][:, :, :, HD:HD + 1], 1.0).then_inc(preset, 1)
                pool.wait_ge(preset, 4)
                for m in range(2):
                    nc.gpsimd.memset(KS[m][64:96, :, :], 1.0).then_inc(ones_in, 1)
                    nc.gpsimd.memset(QS[m][64:96, :, :], 0.0).then_inc(ones_in, 1)
                pool.wait_ge(ones_in, 4)
                for n, name in enumerate("qk"):
                    pool.wait_ge(hi, n + 3)
                    pool.wait_ge(lo, n + 1)
                    nc.gpsimd.tensor_tensor(rest[name], full_qk[name][:, columns(1)], parts[name][:, 0, columns(1)], ALU.subtract).then_inc(resid1, 1)
                for n, name in enumerate("qk"):
                    pool.wait_ge(mid, n + 3)
                    nc.gpsimd.tensor_tensor(parts[name][:, 2, columns(1)], rest[name], parts[name][:, 1, columns(1)], ALU.subtract).then_inc(lo1, 1)
                pool.wait_ge(v_in, 4)

                def own_values(i, par):
                    src = v_all[:, bass.ds(i, 1), :, :].rearrange("p o t (h d) -> p (o t) h d", h=4)
                    nc.gpsimd.tensor_copy(VB[par][:, :, :, 0:HD], src).then_inc(vb_ready, 1)

                own_values(0, 0)
                for t in range(TILES):
                    nc.gpsimd.tensor_tensor(x_tok[:, t, :], x_tok[:, t, :], b_p, ALU.add)

                def body(i, par, has_previous, has_next):
                    if has_next:
                        if has_previous:
                            pool.wait_ge(pv_done, i * n_steps)
                        own_values(i + 1, 1 - par)
                groups(pool, body)

            @block.tensor
            def _(pe):
                def maximum(bank, number, par, unit):
                    hh, qt, kh = unit
                    if not (isinstance(number, int) and number < 2):
                        pe.wait_ge(mx_red, number - 1)
                    keys, masked = keys_of(qt, kh), causal and kh == qt // 4
                    last = nc.tensor.matmul(bank[:, 0:keys], QS[par][0:KROWS, hh, 128 * qt:128 * qt + 128], KS[par][0:KROWS, hh, 512 * kh:512 * kh + keys],
                                            start=True, stop=not masked)
                    if masked:
                        last = nc.tensor.matmul(bank[:, keys - 128:keys], ident_b[:, :], causal_qk[:, :], start=False, stop=True)
                    last.then_inc(mx_full, 1)

                def turn_maxima(half):
                    pe.wait_ge(m_ready, half + 1)
                    if not (isinstance(half, int) and half < 2):
                        pe.wait_ge(o_done, half - 1)
                    nc.tensor.matmul(PS[0:32, 7, 0:128], max_parts_flat, ident_b[:, :], start=True, stop=True).then_inc(mt_full, 1)

                def scores(i, par, n, has_previous):
                    hf, kt = steps[n // 2]
                    if n >= 2 or has_previous:
                        pe.wait_ge(exp_done, i * n_units + n - 1)
                    masked, first_q = causal and kt >= 4 * hf, first_query(hf, kt)
                    for m in range(2):
                        hh = 2 * (n % 2) + m
                        bank = PS[:, 2 * (n % 2) + m, :]
                        last = nc.tensor.matmul(bank[:, first_q:512], KS[par][0:KROWS + 2, hh, 128 * kt:128 * kt + 128],
                                                QS[par][0:KROWS + 2, hh, 512 * hf + first_q:512 * hf + 512], start=True, stop=not masked)
                        if masked:
                            last = nc.tensor.matmul(bank[:, first_q:first_q + 128], ident_b[:, :], causal_kq[:, :], start=False, stop=True)
                    last.then_inc(st_full, 1)

                def values(i, par, s):
                    hf, kt = steps[s]
                    pe.wait_ge(exp_done, i * n_units + 2 * s + 2)
                    if kt == 0 and not (isinstance(i, int) and 2 * i + hf == 0):
                        pe.wait_ge(o_ev, 2 * i + hf)
                    if s == 0:
                        pe.wait_ge(vb_ready, i + 1)
                    first_q = first_query(hf, kt)
                    for hh in range(4):
                        last = nc.tensor.matmul(PS[32 * hh:32 * hh + 32, 6, first_q:512], VB[par][:, kt, hh, :],
                                                PT[(2 * s + hh // 2) % 4][:, 512 * (hh % 2) + first_q:512 * (hh % 2) + 512],
                                                start=kt == 0, stop=s == ends[hf], tile_position=(0, 32 * hh))
                    last.then_inc(pv_done, 1)

                def turn_out(half, hf):
                    pe.wait_ge(o_ev, half + 1)
                    pe.wait_ge(mt_ev, min(half + 2, 2 * HGROUPS) if isinstance(half, int) else half + 2)
                    for t in range(4):
                        last = nc.tensor.transpose(PS[:, 7, 128 * t:128 * t + 128], OT[hf][:, 128 * t:128 * t + 128], ident[:, :])
                    last.then_inc(o_tr, 1)

                if lora:
                    nc.tensor.matmul(PS[:, 6, 0:384], a_qkv_t, b_qkv, start=True, stop=True).then_inc(delta, 1)
                    nc.tensor.matmul(PS[:, 7, 0:128], a_p_t, b_p_lora, start=True, stop=True).then_inc(delta, 1)
                    pe.wait_ge(weights, 2)
                for b in range(B):
                    for n in range(2):
                        for k in range(2):
                            nc.tensor.matmul(PS[:, 4 * b + 2 * n + k, :], w_qkv[:, 128 * n:128 * n + 128], tokens(2 * b + k),
                                             start=True, stop=True).then_inc(mm, 1)
                for k in range(4):
                    pe.wait_ge(evac0, k + 1)
                    for t in range(4):
                        last = nc.tensor.matmul(PS[:, k, 128 * t:128 * t + 128], tokens(k)[:, 128 * t:128 * t + 128], w_qkv[:, 256:384], start=True, stop=True)
                    last.then_inc(mm, 1)
                pe.wait_ge(evac1, 4)
                pe.wait_ge(loaded, LOADS)
                for number, unit in enumerate(max_units[0]):
                    maximum(PS[:, 4 + number % 2, :], number, 0, unit)
                for n, unit in enumerate(max_units[1][:ahead]):
                    number = len(max_units[0]) + n
                    maximum(PS[:, 4 + number % 2, :], number, 0, unit)
                    if n == min(4, ahead - 1):
                        turn_maxima(0)

                def body(i, par, has_previous, has_next):
                    for s in range(n_steps):
                        if has_next and PER * s == own:
                            pe.wait_ge(loaded, LOADS * (i + 2))
                        todo = list(maxima_of_step(i, par, s, has_next))

                        def one_maximum(m):
                            if m < len(todo):
                                n, group_par, unit = todo[m]
                                maximum(PS[:, 4 + n % 2, :], first + i * n_max + n, group_par, unit)
                        if steps[s][1] == 0:
                            pe.wait_ge(rows_in, ROWS * (2 * i + steps[s][0] + 1))
                        one_maximum(0)
                        scores(i, par, 2 * s, has_previous)
                        one_maximum(1)
                        if s:
                            values(i, par, s - 1)
                        elif has_previous:
                            values(i - 1, 1 - par, n_steps - 1)
                        if PER * s == own:
                            turn_maxima(2 * i + 1)
                        if has_next and PER * s == own + len(max_units[0]):
                            turn_maxima(2 * i + 2)
                        one_maximum(2)
                        scores(i, par, 2 * s + 1, has_previous)
                        one_maximum(3)
                        if s == 1 and has_previous:
                            turn_out(2 * i - 1, 1)
                        if s == ends[0] + 2:
                            turn_out(2 * i, 0)
                pe.wait_ge(v_in, 4)
                groups(pe, body)
                values(HGROUPS - 1, 1, n_steps - 1)
                pe.wait_ge(o_done, 2 * HGROUPS - 1)
                turn_out(2 * HGROUPS - 1, 1)

            @block.scalar
            def _(act):
                load_ln_exp()

                def out_half(i, hf):
                    act.wait_ge(pv_done, i * n_steps + ends[hf] + 1)
                    nc.scalar.copy(OT[hf], PS[:, 6, :]).then_inc(o_ev, 1)

                def maxima_rows(half):
                    act.wait_ge(mt_full, half + 1)
                    if not (isinstance(half, int) and half == 0):
                        act.wait_ge(rows_in, ROWS * half)
                    nc.scalar.copy(max_rows, PS[0:32, 7, 0:128]).then_inc(mt_ev, 1)

                for n, name in enumerate("qk"):
                    act.wait_ge(evac0, 2 * n + 2)
                    nc.scalar.copy(parts[name][:, 0, columns(0)], full_qk[name][:, columns(0)]).then_inc(hi, 1)
                for n, name in enumerate("qk"):
                    act.wait_ge(resid, n + 1)
                    nc.scalar.copy(parts[name][:, 1, columns(0)], rest[name]).then_inc(mid, 1)
                act.wait_ge(b_scaled, 1)
                for n, name in enumerate("qk"):
                    for k in range(2):
                        act.wait_ge(mm, 4 + 2 * n + k + 1)
                        nc.scalar.activation(full_qk[name][:, N + 512 * k:N + 512 * k + 512], PS[:, 4 + 2 * n + k, :], ACT.Identity,
                                             scale=HD ** -0.5 if n == 0 else 1.0, bias=b_q_scaled if n == 0 else b_qk[:, 1:2]).then_inc(evac1, 1)
                for n, name in enumerate("qk"):
                    act.wait_ge(evac1, 2 * n + 2)
                    nc.scalar.copy(parts[name][:, 0, columns(1)], full_qk[name][:, columns(1)]).then_inc(hi, 1)
                for n, name in enumerate("qk"):
                    act.wait_ge(resid1, n + 1)
                    nc.scalar.copy(parts[name][:, 1, columns(1)], rest[name]).then_inc(mid, 1)
                maxima_rows(0)

                def body(i, par, has_previous, has_next):
                    for n in range(n_units):
                        s = n // 2
                        if n == 2 and has_previous:
                            out_half(i - 1, 1)
                        if n == 2 * (ends[0] + 1) + 2:
                            out_half(i, 0)
                        if n % 2 and PER * s == own:
                            maxima_rows(2 * i + 1)
                        if n % 2 and has_next and PER * s == own + len(max_units[0]):
                            maxima_rows(2 * i + 2)
                        act.wait_ge(st_full, i * n_units + n + 1)
                        if n >= 4 or has_previous:
                            act.wait_ge(pv_done, i * n_steps + n // 2 - 1)
                        first_q = first_query(*steps[s])
                        nc.scalar.activation(PT[n % 4].rearrange("p (a n) -> p a n", a=2)[:, :, first_q:512], PS[:, 2 * (n % 2):2 * (n % 2) + 2, first_q:512],
                                             ACT.Exp).then_inc(exp_done, 1)
                groups(act, body)
                out_half(HGROUPS - 1, 1)

            @block.vector
            def _(dve):
                nc.vector.memset(maxima, -3.0e38).then_inc(mlink, 1)
                dve.wait_ge(mlink, 1)
                if lora:
                    dve.wait_ge(delta, 2)
                    nc.vector.scalar_tensor_tensor(w_qkv, PS[:, 6, 0:384], 2.0, w_qkv, ALU.mult, ALU.add).then_inc(weights, 1)
                    nc.vector.scalar_tensor_tensor(w_p, PS[:, 7, 0:128], 2.0, w_p, ALU.mult, ALU.add).then_inc(weights, 1)
                nc.vector.tensor_scalar(b_q_scaled, b_qk[:, 0:1], HD ** -0.5, None, ALU.mult).then_inc(b_scaled, 1)
                for n, name in enumerate("qk"):
                    for k in range(2):
                        dve.wait_ge(mm, 2 * n + k + 1)
                        nc.vector.tensor_scalar(full_qk[name][:, 512 * k:512 * k + 512], PS[:, 2 * n + k, :], b_qk[:, n:n + 1],
                                                HD ** -0.5 if n == 0 else 1.0, ALU.add, ALU.mult).then_inc(evac0, 1)
                for n, name in enumerate("qk"):
                    dve.wait_ge(hi, n + 1)
                    nc.vector.tensor_tensor(rest[name], full_qk[name][:, columns(0)], parts[name][:, 0, columns(0)], ALU.subtract).then_inc(resid, 1)
                for n, name in enumerate("qk"):
                    dve.wait_ge(mid, n + 1)
                    nc.vector.tensor_tensor(parts[name][:, 2, columns(0)], rest[name], parts[name][:, 1, columns(0)], ALU.subtract).then_inc(lo, 1)
                for k in range(4):
                    dve.wait_ge(mm, 9 + k)
                    nc.vector.tensor_tensor(v_all[:, 4 * (k // 2):4 * (k // 2) + 4, 4 * (k % 2):4 * (k % 2) + 4, :].rearrange("p g t e -> p t g e"),
                                            PS[:, k, :].rearrange("p (t g e) -> p t g e", t=4, g=4),
                                            b_v.rearrange("p (g e) -> p g e", g=4).unsqueeze(1).broadcast_to([128, 4, 4, 32]), ALU.add).then_inc(v_in, 1)

                def maximum(number, bank, unit):
                    hh, qt, kh = unit
                    dve.wait_ge(mx_full, number + 1)
                    nc.vector.tensor_reduce(maxima[:, hh, qt, kh:kh + 1], bank[:, 0:keys_of(qt, kh)], AX.X, ALU.max).then_inc(mx_red, 1)

                def cut_maxima(half, hf, found):
                    dve.wait_ge(mx_red, found)
                    nc.vector.tensor_reduce(neg_max.unsqueeze(3), maxima[:, :, 4 * hf:4 * hf + 4, :], AX.X, ALU.max,
                                            negate=True).then_inc(mlink, 1)
                    dve.wait_ge(mlink, 3 * half + 2)
                    nc.vector.tensor_copy(max_parts[:, :, 0, :], neg_max).then_inc(mlink, 1)
                    dve.wait_ge(mlink, 3 * half + 3)
                    nc.vector.tensor_tensor(max_rest, neg_max, max_parts[:, :, 0, :], ALU.subtract).then_inc(mlink, 1)
                    dve.wait_ge(mlink, 3 * half + 4)
                    nc.vector.tensor_copy(max_parts[:, :, 1, :], max_rest).then_inc(m_ready, 1)

                def out_half(i, hf):
                    dve.wait_ge(o_tr, 2 * i + hf + 1)
                    o = PS[:, 7, :].rearrange("p (t h d) -> p t h d", t=4, h=4)
                    nc.vector.reciprocal(rden.rearrange("p (t h) -> p t h", t=4).unsqueeze(3), o[:, :, :, HD:HD + 1]).then_inc(o_done_r, 1)
                    dve.wait_ge(o_done_r, 2 * i + hf + 1)
                    dst = o_tok[:, bass.ds(i, 1), 4 * hf:4 * hf + 4, :].rearrange("p o t (h d) -> p (o t) h d", h=4)
                    nc.vector.tensor_tensor(dst, o[:, :, :, 0:HD], rden.rearrange("p (t h) -> p t h", t=4).unsqueeze(3).broadcast_to([128, 4, 4, HD]),
                                            ALU.mult).then_inc(o_done, 1)

                for number, unit in enumerate(max_units[0]):
                    maximum(number, PS[:, 4 + number % 2, :], unit)
                cut_maxima(0, 0, len(max_units[0]))
                for n, unit in enumerate(max_units[1][:ahead]):
                    number = len(max_units[0]) + n
                    maximum(number, PS[:, 4 + number % 2, :], unit)

                def body(i, par, has_previous, has_next):
                    for s in range(n_steps):
                        for n, _, unit in maxima_of_step(i, par, s, has_next):
                            maximum(first + i * n_max + n, PS[:, 4 + n % 2, :], unit)
                        if PER * (s + 1) == own:
                            cut_maxima(2 * i + 1, 1, first + i * n_max + own)
                        if has_next and PER * (s + 1) == own + len(max_units[0]):
                            cut_maxima(2 * i + 2, 0, first + i * n_max + own + len(max_units[0]))
                        if s == 1 and has_previous:
                            out_half(i - 1, 1)
                        if s == ends[0] + 2:
                            out_half(i, 0)
                groups(dve, body)
                out_half(HGROUPS - 1, 1)

        oT = cut(B * N, after_xt)
        o_ord = cut(B * N).rearrange("p (t g d) -> p t g d", t=TILES, g=4)
        with stage("ordered", "turned", "evac", "mm") as (block, ordered, turned, evac, mm):
            @block.tensor
            def _(pe):
                for t in range(TILES):
                    pe.wait_ge(ordered, t // BT + 1)
                    last = nc.tensor.transpose(PS[:, t // 4, 128 * (t % 4):128 * (t % 4) + 128],
                                               o_ord[:, t, :, :].rearrange("p g d -> p (g d)"), ident[:, :])
                    if t % 4 == 3:
                        last.then_inc(turned, 1)
                for k in range(4):
                    pe.wait_ge(evac, k + 1)
                    for t in range(4):
                        last = nc.tensor.matmul(PS[:, 4 + k, 128 * t:128 * t + 128], oT[:, 512 * k + 128 * t:512 * k + 128 * t + 128], w_p, start=True, stop=True)
                    last.then_inc(mm, 1)

            @block.scalar
            def _(act):
                for k in range(4):
                    act.wait_ge(turned, k + 1)
                    nc.scalar.copy(oT[:, 512 * k:512 * k + 512], PS[:, k, :]).then_inc(evac, 1)

            @block.vector
            def _(dve):
                for b in range(B):
                    nc.vector.tensor_copy(o_ord[:, BT * b:BT * b + BT, :, :],
                                          o_tok[:, 4 * b:4 * b + 4, :, :].rearrange("p g t d -> p t g d")).then_inc(ordered, 1)
                for k in range(4):
                    dve.wait_ge(mm, k + 1)
                    xs = x_tok[:, 4 * k:4 * k + 4, :].rearrange("p t c -> p (t c)")
                    nc.vector.tensor_tensor(xs, PS[:, 4 + k, :], xs, ALU.add)


    def rg_lru():
        T = B * N
        sq = cut(T, after_xt)
        h = cut(T)
        gate = [cut(T), cut(T)[0:64, :]]
        up_pad = [cut(B * (N + 3)).rearrange("p (b n) -> p b n", b=B), cut(B * (N + 3)).rearrange("p (b n) -> p b n", b=B)[0:64]]
        uc = [cut(T), cut(T)[0:64, :]]
        ig = [cut(T), cut(T)[0:64, :]]
        alpha = [cut(T), cut(T)[0:64, :]]
        beta = [cut(T), cut(T)[0:64, :]]
        x2, n2, act_up, y_out, rec = h, uc[0], ig, alpha[0], uc

        at = [0]

        def w(n, rows=128):
            at[0] += n
            return wbuf[0:rows, at[0] - n:at[0]]
        w_in, w_gate = w(HID), w(HID)
        w_ig, w_rg = [w(HID), w(HID, 64)], [w(HID), w(HID, 64)]
        w_out = [w(C), w(C, 64)]
        w_mg, w_mu = w(HID), w(HID)
        w_md = [w(C), w(C, 64)]
        vec = [w(8), w(8, 64)]
        norms = w(2)
        lam = w(14)
        M = [(0, 128), (128, 64)]

        loads = []
        for dst, name in ((w_in, "t_W_in"), (w_gate, "t_W_gate"), (w_mg, "t_mlp_gate"), (w_mu, "t_mlp_up")):
            loads.append((dst, I[name]))
        for dst, name in ((w_ig, "t_rg_in"), (w_rg, "t_rg_gate"), (w_out, "t_W_out"), (w_md, "t_mlp_down")):
            for m, (lo, n) in enumerate(M):
                loads.append((dst[m], I[name][lo:lo + n, :]))
        for m, (lo, n) in enumerate(M):
            loads.append((vec[m][:, 0:4], I["conv_w"][lo:lo + n, :]))
            for c, name in enumerate(("L1_attn_a_conv_b", "L1_attn_a_rg_in_b", "L1_attn_a_rg_gate_b", "L1_attn_a_forget_lambda")):
                loads.append((vec[m][:, 4 + c:5 + c], I[name][lo:lo + n].rearrange("(p o) -> p o", o=1)))
        for m, name in enumerate(("L1_attn_a_norm1_w", "L1_attn_a_norm2_w")):
            loads.append((norms[:, m:m + 1], I[name].rearrange("(p o) -> p o", o=1)))

        def q(buf, k):
            return buf[:, 512 * k:512 * k + 512]

        layernorm_to_xt(loads)
        names = ("padded", "alink", "dlink", "sp_y", "sq1", "p_ms1", "rs1", "h_ready", "p_u", "e_u", "u_conv", "p_gate", "e_gate",
                 "p_ig", "e_ig", "p_rg", "e_rg", "sp_ready", "a_ready", "a_sq", "one_m", "b_ready", "m_ready", "p_mix", "e_mix", "sq2",
                 "p_ms2", "rs2", "n2_ready", "p_mg", "e_mg", "p_mu", "e_mu", "p_md", "e_md", "p_tr")
        with stage(*names) as (block, *sems):
            S = dict(zip(names, sems))
            @block.gpsimd
            def _(pool):
                for m in range(2):
                    nc.gpsimd.memset(up_pad[m][:, :, 0:3], 0.0).then_inc(S["padded"], 1)
                nc.gpsimd.memset(lam, 0.0).then_inc(S["padded"], 1)

            @block.tensor
            def _(pe):
                def sums(src, ready, done, bank):
                    for k in range(4):
                        pe.wait_ge(ready, k + 1)
                        nc.tensor.matmul(PS[:, bank + k, :], ones[:, :], q(src, k), start=True, stop=True).then_inc(done, 1)

                def expand(weights, src, ready, free, done):
                    for m, (lo, n) in enumerate(M):
                        for k in range(4):
                            pe.wait_ge(ready, k + 1)
                            if free is not None:
                                pe.wait_ge(free, 4 * m + k + 1)
                            nc.tensor.matmul(PS[0:n, 4 * m + k, :], weights[:, lo:lo + n], q(src, k), start=True, stop=True).then_inc(done, 1)

                def square_mm(weights, src, done, free):
                    for m, (lo, n) in enumerate(M):
                        for k in range(4):
                            pe.wait_ge(free, 4 * m + k + 1)
                            nc.tensor.matmul(PS[0:n, 4 * m + k, :], weights[0][:, lo:lo + n], q(src[0], k), start=True, stop=False)
                            nc.tensor.matmul(PS[0:n, 4 * m + k, :], weights[1][:, lo:lo + n], q(src[1], k), start=False, stop=True).then_inc(done, 1)

                def reduce_mm(weights, src, done):
                    for k in range(4):
                        nc.tensor.matmul(PS[:, k, :], weights[0], q(src[0], k), start=True, stop=False)
                        nc.tensor.matmul(PS[:, k, :], weights[1], q(src[1], k), start=False, stop=True).then_inc(done, 1)

                sums(sq, S["sq1"], S["p_ms1"], 0)
                pe.wait_ge(S["rs1"], 4)
                expand(w_in, h, S["h_ready"], None, S["p_u"])
                expand(w_gate, h, S["h_ready"], S["e_u"], S["p_gate"])
                pe.wait_ge(S["u_conv"], 2)
                square_mm(w_ig, uc, S["p_ig"], S["e_gate"])
                square_mm(w_rg, uc, S["p_rg"], S["e_ig"])
                pe.wait_ge(S["e_rg"], 8)
                pe.wait_ge(S["m_ready"], 2)
                reduce_mm(w_out, gate, S["p_mix"])
                sums(sq, S["sq2"], S["p_ms2"], 4)
                pe.wait_ge(S["rs2"], 4)
                expand(w_mg, n2, S["n2_ready"], None, S["p_mg"])
                expand(w_mu, n2, S["n2_ready"], S["e_mg"], S["p_mu"])
                pe.wait_ge(S["e_mu"], 8)
                reduce_mm(w_md, act_up, S["p_md"])
                for k in range(4):
                    pe.wait_ge(S["e_md"], k + 1)
                    for t in range(4):
                        last = nc.tensor.transpose(PS[:, 4 + k, 128 * t:128 * t + 128], q(y_out, k)[:, 128 * t:128 * t + 128], ident[:, :])
                    last.then_inc(S["p_tr"], 1)

            @block.scalar
            def _(act):
                link = linker(act, S["alink"])
                load_ln_exp()
                act.wait_ge(S["sp_y"], 1)
                nc.scalar.activation(lam[:, 4:6], lam[:, 2:4], ACT.Exp, scale=-1.0).then_inc(S["sp_y"], 1)
                for k in range(4):
                    nc.scalar.activation(q(sq, k), tokens(k), ACT.Square).then_inc(S["sq1"], 1)

                def rsqrt_mean(bank, done_in, done):
                    for k in range(4):
                        act.wait_ge(done_in, k + 1)
                        link(nc.scalar.activation(q(sq, k), PS[:, bank + k, :], ACT.Ln, scale=1.0 / C, bias=eps_ap))
                        nc.scalar.activation(q(sq, k), q(sq, k), ACT.Exp, scale=-0.5).then_inc(done, 1)
                rsqrt_mean(0, S["p_ms1"], S["rs1"])

                def both(func, done_in, dst, done, bias=None):
                    for m, (lo, n) in enumerate(M):
                        for k in range(4):
                            act.wait_ge(done_in, 4 * m + k + 1)
                            args = {} if bias is None else {"bias": vec[m][:, bias:bias + 1]}
                            nc.scalar.activation(q(dst[m], k), PS[0:n, 4 * m + k, :], func, **args).then_inc(done, 1)
                both(ACT.Gelu, S["p_gate"], gate, S["e_gate"])
                both(ACT.Sigmoid, S["p_ig"], ig, S["e_ig"], 5)
                both(ACT.Sigmoid, S["p_rg"], alpha, S["e_rg"], 6)
                act.wait_ge(S["sp_ready"], 1)
                act.wait_ge(S["e_rg"], 8)
                for m, (lo, n) in enumerate(M):
                    nc.scalar.activation(alpha[m], alpha[m], ACT.Exp, scale=lam[0:n, 12 + m:13 + m]).then_inc(S["a_ready"], 1)
                for m in range(2):
                    act.wait_ge(S["a_ready"], m + 1)
                    nc.scalar.activation(beta[m], alpha[m], ACT.Square).then_inc(S["a_sq"], 1)
                for m, (lo, n) in enumerate(M):
                    act.wait_ge(S["one_m"], m + 1)
                    nc.scalar.activation(beta[m], beta[m], ACT.Sqrt, bias=rms_eps[0:n, :]).then_inc(S["b_ready"], 1)
                for k in range(4):
                    act.wait_ge(S["e_mix"], k + 1)
                    nc.scalar.activation(q(sq, k), q(x2, k), ACT.Square).then_inc(S["sq2"], 1)
                load_ln_exp()
                rsqrt_mean(4, S["p_ms2"], S["rs2"])
                both(ACT.Gelu, S["p_mg"], act_up, S["e_mg"])

            @block.vector
            def _(dve):
                link = linker(dve, S["dlink"])
                dve.wait_ge(S["padded"], 3)
                for m, (lo, n) in enumerate(M):
                    link(nc.vector.tensor_copy(lam[0:n, m:m + 1], vec[m][:, 7:8]))
                link(nc.vector.tensor_scalar(lam[:, 2:4], lam[:, 0:2], -1.0, None, ALU.mult))
                nc.vector.tensor_tensor(lam[:, 2:4], lam[:, 2:4], lam[:, 0:2], ALU.max).then_inc(S["sp_y"], 1)
                dve.wait_ge(S["sp_y"], 2)
                link(nc.vector.tensor_scalar(lam[:, 6:8], lam[:, 4:6], 2.0, None, ALU.add))
                link(nc.vector.reciprocal(lam[:, 6:8], lam[:, 6:8]))
                link(nc.vector.tensor_tensor(lam[:, 6:8], lam[:, 6:8], lam[:, 4:6], ALU.mult))
                link(nc.vector.tensor_tensor(lam[:, 8:10], lam[:, 6:8], lam[:, 6:8], ALU.mult))
                link(nc.vector.tensor_scalar(lam[:, 10:12], lam[:, 8:10], 1.0 / 17, None, ALU.mult))
                for odd in range(15, 1, -2):
                    link(nc.vector.scalar_tensor_tensor(lam[:, 10:12], lam[:, 10:12], 1.0 / odd, lam[:, 8:10], ALU.add, ALU.mult))
                link(nc.vector.scalar_tensor_tensor(lam[:, 10:12], lam[:, 10:12], 1.0, lam[:, 6:8], ALU.add, ALU.mult))
                link(nc.vector.tensor_scalar(lam[:, 12:14], lam[:, 0:2], 0.0, -8.0, ALU.max, ALU.mult))
                nc.vector.scalar_tensor_tensor(lam[:, 12:14], lam[:, 10:12], -16.0, lam[:, 12:14], ALU.mult, ALU.add).then_inc(S["sp_ready"], 1)

                for k in range(4):
                    dve.wait_ge(S["rs1"], k + 1)
                    nc.vector.scalar_tensor_tensor(q(h, k), tokens(k), norms[:, 0:1], q(sq, k), ALU.mult, ALU.mult).then_inc(S["h_ready"], 1)
                for m, (lo, n) in enumerate(M):
                    for k in range(4):
                        dve.wait_ge(S["p_u"], 4 * m + k + 1)
                        b, c = k // 2, 3 + 512 * (k % 2)
                        nc.vector.tensor_copy(up_pad[m][:, b, c:c + 512], PS[0:n, 4 * m + k, :]).then_inc(S["e_u"], 1)
                dve.wait_ge(S["e_u"], 8)
                for m in range(2):
                    d = uc[m].rearrange("p (b n) -> p b n", b=B)
                    link(nc.vector.tensor_scalar(d, up_pad[m][:, :, 0:N], vec[m][:, 0:1], vec[m][:, 4:5], ALU.mult, ALU.add))
                    for tap in (1, 2, 3):
                        ins = nc.vector.scalar_tensor_tensor(d, up_pad[m][:, :, tap:tap + N], vec[m][:, tap:tap + 1], d, ALU.mult, ALU.add)
                        if tap < 3:
                            link(ins)
                        else:
                            ins.then_inc(S["u_conv"], 1)
                for m in range(2):
                    dve.wait_ge(S["a_sq"], m + 1)
                    nc.vector.tensor_scalar(beta[m], beta[m], -1.0, 1.0, ALU.mult, ALU.add).then_inc(S["one_m"], 1)
                dve.wait_ge(S["u_conv"], 2)
                for m in range(2):
                    link(nc.vector.tensor_tensor(ig[m], ig[m], uc[m], ALU.mult))
                for m in range(2):
                    dve.wait_ge(S["b_ready"], m + 1)
                    link(nc.vector.tensor_tensor(beta[m], beta[m], ig[m], ALU.mult))
                    for b in range(B):
                        r = slice(N * b, N * b + N)
                        link(nc.vector.tensor_tensor_scan(rec[m][:, r], alpha[m][:, r], beta[m][:, r], 0.0, ALU.mult, ALU.add))
                    nc.vector.tensor_tensor(gate[m], gate[m], rec[m], ALU.mult).then_inc(S["m_ready"], 1)
                for k in range(4):
                    dve.wait_ge(S["p_mix"], k + 1)
                    nc.vector.tensor_tensor(q(x2, k), PS[:, k, :], tokens(k), ALU.add).then_inc(S["e_mix"], 1)
                for k in range(4):
                    dve.wait_ge(S["rs2"], k + 1)
                    if k == 0:
                        dve.wait_ge(S["m_ready"], 2)
                    nc.vector.scalar_tensor_tensor(q(n2, k), q(x2, k), norms[:, 1:2], q(sq, k), ALU.mult, ALU.mult).then_inc(S["n2_ready"], 1)
                for m, (lo, n) in enumerate(M):
                    for k in range(4):
                        dve.wait_ge(S["p_mu"], 4 * m + k + 1)
                        nc.vector.tensor_tensor(q(act_up[m], k), PS[0:n, 4 * m + k, :], q(act_up[m], k), ALU.mult).then_inc(S["e_mu"], 1)
                for k in range(4):
                    dve.wait_ge(S["p_md"], k + 1)
                    nc.vector.tensor_tensor(q(y_out, k), PS[:, k, :], q(x2, k), ALU.add).then_inc(S["e_md"], 1)
                for k in range(4):
                    dve.wait_ge(S["p_tr"], k + 1)
                    xs = x_tok[:, 4 * k:4 * k + 4, :].rearrange("p t c -> p (t c)")
                    nc.vector.tensor_tensor(xs, PS[:, 4 + k, :], xs, ALU.add)


    def shifted_evac(k, bank):
        b, lo, n = k // 2, PAD + 512 * (k % 2), 511 if k % 2 else 512
        nc.scalar.copy(XT[0:64, b, lo:lo + 512], PS[0:64, bank, :])
        return nc.scalar.copy(XT[64:128, b, lo + 1:lo + 1 + n], PS[64:128, bank, 0:n])

    def window_layers():
        qz = cut(2 * B * XW, after_xt).rearrange("p (h b n) -> p h b n", h=2, b=B)
        kT = cut(B * XW).rearrange("p (b n) -> p b n", b=B)
        qz_b = cut(B * XW).bitcast(BF16).rearrange("p (h b n) -> p h b n", h=2, b=B)
        kT_b = cut(B * XW // 2).bitcast(BF16).rearrange("p (b n) -> p b n", b=B)
        oT = cut(B * QW).rearrange("p (b n) -> p b n", b=B)
        v_tok = cut(2 * CHUNKS * 128).rearrange("p (c n) -> p c n", n=128)
        raw_at = Cut.at
        raw = cut(TILES * 256).rearrange("p (t n) -> p t n", t=TILES)
        rot_at = Cut.at
        rot = cut(TILES * 256).rearrange("p (t n) -> p t n", t=TILES)
        cross = cut(1024)
        squares = cut(1024)
        base_a, base_b, tab_a, tab_b = (cut(BT * 128) for _ in range(4))
        scales = cut(128)
        swapped = cut(128)
        PT = [cut(4 * QC) for _ in range(2)]
        log_den = [cut(2 * QC) for _ in range(2)]
        rec_den = [cut(2 * QC) for _ in range(2)]
        neg_max = [cut(4) for _ in range(4)]
        gate = cut(2)
        norms2 = cut(16)
        inv_norm = cut(16)
        w_qk, w_v, w_o = wbuf[:, 0:256], wbuf[:, 256:384], wbuf[:, 384:512]
        xn_tok = arena[:, raw_at:raw_at + B * N].rearrange("p (t c) -> p t c", t=TILES)
        xnT = arena[:, raw_at + B * N:raw_at + 2 * B * N]
        uT = [arena[:, rot_at + n * B * N:rot_at + (n + 1) * B * N] for n in range(3)]
        gated = [v_tok.rearrange("p c n -> p (c n)")[:, 512 * n:512 * n + 512] for n in range(2)]
        FF = [(0, 128), (128, 128), (256, INNER - 256)]

        with stage("stat", "lnv", "rs", "loaded", "kept") as (block, stat, lnv, rs, loaded, kept):
            @block.sync
            def _(sp):
                sp.dma_start(base_a, I["c_rot_a"]).then_inc(loaded, 16)
                sp.dma_start(base_b, I["c_rot_b"]).then_inc(loaded, 16)
                sp.wait_ge(loaded, 32)

            @block.gpsimd
            def _(pool):
                for z in (qz, kT, qz_b, kT_b):
                    nc.gpsimd.memset(z, 0.0)

            @block.vector
            def _(dve):
                nc.vector.memset(XT[64:128, :, PAD:PAD + 1], 0.0)
                nc.vector.tensor_copy(x_keep[:, :, :], x_tok[:, :, :]).then_inc(kept, 1)
                for t in range(TILES):
                    nc.vector.bn_stats(stats[:, t, :], x_tok[:, t, :]).then_inc(stat, 1)
                for t in range(TILES):
                    dve.wait_ge(stat, t + 1)
                    nc.vector.bn_aggr(moments[:, t, :], stats[:, t, :]).then_inc(stat, 1)
                dve.wait_ge(rs, 1)
                dve.wait_ge(kept, 1)
                for t in range(TILES):
                    nc.vector.tensor_scalar(x_tok[:, t, :], x_keep[:, t, :], moments[:, t, 0:1], rstd[:, t:t + 1], ALU.subtract, ALU.mult)

            @block.scalar
            def _(act):
                load_ln_exp()
                act.wait_ge(stat, 2 * TILES)
                nc.scalar.activation(rstd[:, :], moments[:, :, 1], ACT.Ln, bias=eps_ap).then_inc(lnv, 1)
                act.wait_ge(lnv, 1)
                nc.scalar.activation(rstd[:, :], rstd[:, :], ACT.Exp, scale=-0.5).then_inc(rs, 1)

        with nc.Fori(0, DEPTH) as layer:
            with stage("full", "free0", "free1", "mx_full", "mx_red", "d_ready", "st_full", "exp_done", "pv_full", "ln_done", "den_done",
                       "o_done", "sq_done", "n2_ready", "t1_done", "t2_done", "add_done", "ln2_done", "rn_ready", "rot_done",
                       "wqk_in", "wv_in", "wo_in", "ff_in", "red_done", "cast_done", "scales_in", "turned", "xt_in", "tables", "x_split", "w_split", "w1_split", "xn_high", "xn_low",
                       "ff_turned", "shifted", "back", "stat", "lnv", "rs", "normed", "turned2", "xn_in", "gate_mm", "a_mm", "gelu_done", "u_done",
                       "y_mm", "b2_added") as (
                    block, full, free0, free1, mx_full, mx_red, d_ready, st_full, exp_done, pv_full, ln_done, den_done,
                    o_done, sq_done, n2_ready, t1_done, t2_done, add_done, ln2_done, rn_ready, rot_done,
                    wqk_in, wv_in, wo_in, ff_in, red_done, cast_done, scales_in, turned, xt_in, tables, x_split, w_split, w1_split, xn_high, xn_low,
                    ff_turned, shifted, back, stat, lnv, rs, normed, turned2, xn_in, gate_mm, a_mm, gelu_done, u_done,
                    y_mm, b2_added):
                free = (free0, free1)
                STEPS = CHUNKS + 4
                QUARTERS = (0, 2, 1, 3)
                LATE = {8: ("T0", "T1"), 9: ("T2", "T3"), 10: ("V0",), 11: ("V1", "V2"), 12: ("T4", "V3"), 13: ("T5",),
                        STEPS: ("V4", "V5", "T6", "T7", "Y0", "Y1", "Y2", "Y3")}
                FILL_ORDER = tuple(range(8)) + tuple(name for step in sorted(LATE) for name in LATE[step])
                FILLS = len(FILL_ORDER)

                def is_output(name):
                    return name in ("Y0", "Y1", "Y2", "Y3")

                def fill(p, name):
                    if isinstance(p, int) and p == 0:
                        return [f for f in FILL_ORDER if not is_output(f)].index(name)
                    if isinstance(p, int) and p == PAIRS:
                        return FILLS * p - 4 + int(name[1])
                    return FILLS * p - 4 + FILL_ORDER.index(name)

                def before(p, name):
                    if isinstance(p, int):
                        return fill(p, name) // 2
                    return (FILLS // 2) * p + FILL_ORDER.index(name) // 2 - 2

                def bank_of(name):
                    return FILL_ORDER.index(name) % 2

                for p in (0, PAIRS):
                    assert all(fill(p, name) % 2 == bank_of(name) for name in FILL_ORDER if is_output(name) == (p == PAIRS))

                def iterations(eng, body):
                    body(0, True, False)
                    with eng.Fori(1, PAIRS) as p:
                        body(p, True, True)
                    body(PAIRS, False, True)

                def unit(b, h):
                    return 2 * b + h

                items = [(k, n) for k in range(4) for n in range(3)]

                @block.sync
                def _(sp):
                    sp.dma_start(w_qk, I["w_pairs"][bass.ds(layer * PAIRS, 1), :, 0:256].rearrange("o p n -> (o p) n")).then_inc(wqk_in, 16)
                    for n, name in enumerate(("L1_ffn_q_scale", "L1_ffn_k_scale")):
                        src = I[name][bass.ds(layer, 1), :]
                        for dst, lo, at in ((scales, 0, 64 * n), (scales, 32, 64 * n + 32), (swapped, 32, 64 * n), (swapped, 0, 64 * n + 32)):
                            sp.dma_start(dst[:, at:at + 32], src[:, lo:lo + 32].broadcast_to([128, 32])).then_inc(scales_in, 16)
                    sp.dma_start(w_v, I["w_pairs"][bass.ds(layer * PAIRS, 1), :, 256:384].rearrange("o p n -> (o p) n")).then_inc(wv_in, 16)
                    sp.dma_start(w1[:, :], I["L1_ffn_W1"][bass.ds(layer, 1), :, :].rearrange("o p n -> (o p) n")).then_inc(ff_in, 16)
                    for n, (lo, width) in enumerate(FF):
                        sp.dma_start(w2[0:width, n, :], I["L1_ffn_W2"][bass.ds(layer, 1), lo:lo + width, :].rearrange("o p n -> (o p) n")).then_inc(ff_in, 16)
                    sp.dma_start(ff_cols[:, :], I["ff_cols"][bass.ds(layer, 1), :, :].rearrange("o p n -> (o p) n")).then_inc(ff_in, 16)
                    sp.dma_start(b2_row[:, :], I["L1_ffn_b2"][bass.ds(layer, 1), :].broadcast_to([128, C])).then_inc(ff_in, 16)

                    def out_weights(p):
                        sp.dma_start(w_o, I["w_out_pairs"][bass.ds(layer * PAIRS + p, 1), :, :].rearrange("o p n -> (o p) n")).then_inc(wo_in, 16)

                    with sp.Fori(1, PAIRS) as p:
                        src = I["w_pairs"][bass.ds(layer * PAIRS + p, 1), :, :].rearrange("o p n -> (o p) n")
                        sp.wait_ge(full, FILLS * p - 18)
                        sp.dma_start(w_qk, src[:, 0:256]).then_inc(wqk_in, 16)
                        sp.wait_ge(full, FILLS * p - 4)
                        sp.dma_start(w_v, src[:, 256:384]).then_inc(wv_in, 16)
                        out_weights(p - 1)
                    sp.wait_ge(full, FILLS * PAIRS - 4)
                    out_weights(PAIRS - 1)
                    sp.wait_ge(ff_in, 6 * 16)

                @block.tensor
                def _(pe):
                    def maximum(r, g):
                        if g >= 2:
                            pe.wait_ge(mx_red, r * CHUNKS + (g - 1))
                        if g == 0:
                            pe.wait_ge(cast_done, 8 * r + 4)
                        if QC * g + 128 > PAD + 512 >= QC * (g - 1) + 128:
                            pe.wait_ge(cast_done, 8 * r + 8)
                        bank = PS[0:QC, 2 + g % 2, :]
                        for b in range(B):
                            for h in range(2):
                                last = nc.tensor.matmul(bank[:, 128 * unit(b, h):128 * unit(b, h) + 128], qz_b[:, h, b, QC * g:QC * g + QC],
                                                        kT_b[:, b, QC * g:QC * g + 128], start=True, stop=True)
                        last.then_inc(mx_full, 1)

                    def scores(r, g):
                        pe.wait_ge(d_ready, r * CHUNKS + (g + 1))
                        if g >= 2:
                            pe.wait_ge(exp_done, r * CHUNKS + (g - 1))
                        bank = PS[:, 4 + g % 2, 0:4 * QC]
                        nc.tensor.matmul(bank, ident_b[:, :], band_kq[g == 0][:, :].unsqueeze(1).broadcast_to([128, 4, QC]), start=True, stop=False)
                        nc.tensor.matmul(bank, ones_r[0:QC, :], diag[g % 3][0:QC, :], start=False, stop=False)
                        for b in range(B):
                            last = nc.tensor.matmul(bank[:, 2 * QC * b:2 * QC * b + 2 * QC], kT[:, b, QC * g:QC * g + 128],
                                                    qz[:, :, b, QC * g:QC * g + QC], start=False, stop=b == 1)
                        last.then_inc(st_full, 1)

                    def values(r, g):
                        pe.wait_ge(exp_done, r * CHUNKS + (g + 1))
                        if g >= 2:
                            pe.wait_ge(o_done, r * CHUNKS + (g - 1))
                        for b in range(B):
                            for h in range(2):
                                nc.tensor.matmul(PS[64 * h:64 * h + 64, 6 + g % 2, QC * b:QC * b + QC], v_tok[:, 2 * g + b, 64 * h:64 * h + 64],
                                                 PT[g % 2][:, QC * unit(b, h):QC * unit(b, h) + QC], start=True, stop=True, tile_position=(0, 64 * h))
                        for h in range(2):
                            last = nc.tensor.matmul(PS[64 * h:64 * h + 64, 6 + g % 2, 2 * QC:4 * QC], ones[:, 0:64],
                                                    PT[g % 2].rearrange("p (b h n) -> p b h n", b=B, h=2)[:, :, h, :], start=True, stop=True, tile_position=(0, 64 * h))
                        last.then_inc(pv_full, 1)

                    def fill_bank(p, name, items, f):
                        pe.wait_ge(free[bank_of(name)], before(p, name))
                        for j in range(items):
                            last = f(j, PS[:, bank_of(name), :])
                        last.then_inc(full, 1)

                    def late_fills(p, s, a, bb):
                        for name in LATE.get(s, ()):
                            f = int(name[1])
                            if not (bb if is_output(name) else a):
                                continue
                            if name == "V0":
                                pe.wait_ge(wv_in, 16 * p + 16)
                                pe.wait_ge(xt_in, 4)
                            if name == "Y0":
                                pe.wait_ge(wo_in, 16 * p)
                                pe.wait_ge(o_done, p * CHUNKS)
                            if name[0] == "V":
                                def part(j, bank, f=f):
                                    c, b = (4 * f + j) // 2, (4 * f + j) % 2
                                    return nc.tensor.matmul(bank[:, 128 * j:128 * j + 128], XT[:, b, QC * c:QC * c + 128], w_v, start=True, stop=True)
                            elif name[0] == "Y":
                                def part(j, bank, f=f):
                                    t = 4 * f + j
                                    return nc.tensor.matmul(bank[:, 128 * j:128 * j + 128], oT[:, t // BT, 128 * (t % BT):128 * (t % BT) + 128], w_o,
                                                            start=True, stop=True)
                            else:
                                pe.wait_ge(rot_done, 4 * p + (f // 2 + 1))

                                def part(j, bank, quarter=QUARTERS[f // 2], lo=0 if f % 2 else 128):
                                    return nc.tensor.transpose(bank[:, 128 * j:128 * j + 128], rot[:, 4 * quarter + j, lo:lo + 128], ident[:, :])
                            fill_bank(p, name, 2 if name == "V5" else 4, part)

                    def body(p, a, bb):
                        r = p - 1
                        if a:
                            pe.wait_ge(w_split, 2 * p + 2)
                        for s in range(STEPS):
                            if bb and s < CHUNKS:
                                maximum(r, s)
                            if a and s < 8:
                                def qk(j, bank, s=s):
                                    t = 4 * QUARTERS[s // 2] + 2 * (s % 2) + j
                                    if isinstance(p, int) and s % 2 == 0 and j == 0:
                                        pe.wait_ge(x_split, 2 * (s // 2) + 2)
                                    for n, (i, m) in enumerate(PRODUCTS):
                                        last = nc.tensor.matmul(bank[:, 256 * j:256 * j + 256], x_parts[i][:, 128 * t:128 * t + 128], w_parts[m][:, :],
                                                                start=n == 0, stop=n == 2)
                                    return last
                                fill_bank(p, s, 2, qk)
                            if bb and 0 <= s - 2 < CHUNKS:
                                scores(r, s - 2)
                            if bb and 0 <= s - 3 < CHUNKS:
                                values(r, s - 3)
                            late_fills(p, s, a, bb)
                        late_fills(p, STEPS, a, bb)

                    for n, k in enumerate(QUARTERS):
                        for t in range(4):
                            last = nc.tensor.transpose(PS[:, 4 + n, 128 * t:128 * t + 128], x_tok[:, 4 * k + t, :], ident[:, :])
                        last.then_inc(turned, 1)
                    iterations(pe, body)

                    for name in ("Y2", "Y3"):
                        pe.wait_ge(free[bank_of(name)], before(PAIRS, name) + 1)
                    pe.wait_ge(ff_in, 6 * 16)
                    for t in range(TILES):
                        nc.tensor.transpose(PS[:, t // 4, 128 * (t % 4):128 * (t % 4) + 128], x_tok[:, t, :], ident[:, :]).then_inc(ff_turned, 1)
                    for k in range(4):
                        pe.wait_ge(shifted, k + 1)
                        for t in range(4):
                            nc.tensor.transpose(PS[:, 4 + k, 128 * t:128 * t + 128], tokens(k)[:, 128 * t:128 * t + 128], ident[:, :]).then_inc(back, 1)

                    def turn_normed(k):
                        pe.wait_ge(normed, 4 * k + 4)
                        for t in range(4):
                            nc.tensor.transpose(PS[:, 4 + k, 128 * t:128 * t + 128], xn_tok[:, 4 * k + t, :], ident[:, :]).then_inc(turned2, 1)

                    def y(k):
                        pe.wait_ge(u_done, 3 * k + 3)
                        for t in range(4):
                            lo = 512 * k + 128 * t
                            for n, (_, width) in enumerate(FF):
                                last = nc.tensor.matmul(PS[:, 4 + k, 128 * t:128 * t + 128], uT[n][0:width, lo:lo + 128], w2[0:width, n, :], start=n == 0, stop=n == 2)
                        last.then_inc(y_mm, 1)

                    turn_normed(0)
                    for i, (k, n) in enumerate(items):
                        lo, width = FF[n]
                        if n == 0:
                            if k < 3:
                                turn_normed(k + 1)
                            pe.wait_ge(xn_low, k + 1)
                            pe.wait_ge(w1_split, 2)
                        if i >= 2:
                            pe.wait_ge(gelu_done, i - 1)
                            pe.wait_ge(u_done, i - 1)
                        for bank, at, made in ((i % 2, INNER + lo, gate_mm), (2 + i % 2, lo, a_mm)):
                            for m, (wp, xp) in enumerate(PRODUCTS):
                                last = nc.tensor.matmul(PS[0:width, bank, :], w1_parts[wp][:, at:at + width], x_parts[xp][:, 512 * k:512 * k + 512],
                                                        start=m == 0, stop=m == 2)
                            last.then_inc(made, 1)
                        if n == 1 and k:
                            y(k - 1)
                    y(3)

                @block.scalar
                def _(act):
                    load_ln_exp()

                    def exps(r, g):
                        act.wait_ge(st_full, r * CHUNKS + (g + 1))
                        if g >= 2:
                            act.wait_ge(pv_full, r * CHUNKS + (g - 1))
                        nc.scalar.activation(PT[g % 2], PS[:, 4 + g % 2, 0:4 * QC], ACT.Exp).then_inc(exp_done, 1)

                    def denominators(r, g):
                        act.wait_ge(pv_full, r * CHUNKS + (g + 1))
                        if g >= 2:
                            act.wait_ge(o_done, r * CHUNKS + (g - 1))
                        nc.scalar.activation(log_den[g % 2], PS[:, 6 + g % 2, 2 * QC:4 * QC], ACT.Ln).then_inc(ln_done, 1)
                        act.wait_ge(ln_done, r * CHUNKS + (g + 1))
                        nc.scalar.activation(rec_den[g % 2], log_den[g % 2], ACT.Exp, scale=-1.0).then_inc(den_done, 1)

                    def late_copies(p, s):
                        for name in LATE.get(s, ()):
                            if is_output(name):
                                continue
                            f, bank, bank_free = int(name[1]), PS[:, bank_of(name), :], free[bank_of(name)]
                            act.wait_ge(full, fill(p, name) + 1)
                            if name[0] == "V":
                                n = 4 if f < 5 else 2
                                nc.scalar.copy(v_tok[:, 4 * f:4 * f + n, :].rearrange("p c n -> p (c n)"), bank[:, 0:128 * n]).then_inc(bank_free, 1)
                                continue
                            b, lo = QUARTERS[f // 2] // 2, 512 * (QUARTERS[f // 2] % 2)
                            if f % 2:
                                nc.scalar.copy(qz[0:64, 0, b, lo:lo + 512], bank[0:64, :])
                                nc.scalar.copy(qz[64:128, 1, b, lo:lo + 512], bank[64:128, :]).then_inc(bank_free, 1)
                            else:
                                nc.scalar.copy(kT[:, b, PAD + lo:PAD + lo + 512], bank).then_inc(bank_free, 1)

                    def body(p, a, bb):
                        r = p - 1
                        for s in range(STEPS):
                            if a and s < 8:
                                t = 4 * QUARTERS[s // 2] + 2 * (s % 2)
                                act.wait_ge(full, fill(p, s) + 1)
                                nc.scalar.copy(raw[:, t:t + 2, :].rearrange("p t n -> p (t n)"), PS[:, s % 2, :]).then_inc(free[s % 2], 1)
                            if a and s % 3 == 1 and s // 3 < 4:
                                i, quarter = s // 3, QUARTERS[s // 3]
                                act.wait_ge(free[1], before(p, 2 * i + 1) + 1)
                                act.wait_ge(free[0], before(p, 2 * i) + 1)
                                act.wait_ge(red_done, 4 * p + i)
                                nc.scalar.activation(squares, raw[:, 4 * quarter:4 * quarter + 4, :].rearrange("p t n -> p (t n)"), ACT.Square).then_inc(sq_done, 1)
                            if a and s % 3 == 0 and 1 <= s // 3 <= 4:
                                i = s // 3 - 1
                                act.wait_ge(n2_ready, 4 * p + (i + 1))
                                act.wait_ge(rot_done, 4 * p + i)
                                nc.scalar.activation(inv_norm, norms2, ACT.Ln, scale=65536.0).then_inc(ln2_done, 1)
                                act.wait_ge(ln2_done, 4 * p + (i + 1))
                                nc.scalar.activation(inv_norm, inv_norm, ACT.Exp, scale=-0.5, bias=ln256).then_inc(rn_ready, 1)
                            if bb and 0 <= s - 2 < CHUNKS:
                                exps(r, s - 2)
                            if bb and 0 <= s - 3 < CHUNKS:
                                denominators(r, s - 3)
                            if a:
                                late_copies(p, s)
                        if a:
                            late_copies(p, STEPS)

                    for n, k in enumerate(QUARTERS):
                        act.wait_ge(turned, n + 1)
                        shifted_evac(k, 4 + n).then_inc(xt_in, 1)
                    iterations(act, body)

                    act.wait_ge(ff_in, 6 * 16)
                    for k in range(4):
                        act.wait_ge(ff_turned, 4 * k + 4)
                        shifted_evac(k, k).then_inc(shifted, 1)

                    def rstd_of(k):
                        r = rstd[:, 4 * k:4 * k + 4]
                        act.wait_ge(stat, 8 * k + 8)
                        nc.scalar.activation(r, moments[:, 4 * k:4 * k + 4, 1], ACT.Ln, bias=eps_ap).then_inc(lnv, 1)
                        act.wait_ge(lnv, k + 1)
                        nc.scalar.activation(r, r, ACT.Exp, scale=-0.5).then_inc(rs, 1)

                    def normed_in(k):
                        act.wait_ge(turned2, 4 * k + 4)
                        nc.scalar.activation(xnT[:, 512 * k:512 * k + 512], PS[:, 4 + k, :], ACT.Identity, scale=ff_cols[:, 6:7], bias=ff_cols[:, 7:8]).then_inc(xn_in, 1)
                        nc.scalar.activation(x_parts[0][:, 512 * k:512 * k + 512], PS[:, 4 + k, :], ACT.Identity, scale=ff_cols[:, 6:7], bias=ff_cols[:, 7:8]).then_inc(xn_high, 1)

                    rstd_of(0)
                    rstd_of(1)
                    normed_in(0)
                    rstd_of(2)
                    rstd_of(3)
                    for i, (k, n) in enumerate(items):
                        lo, width = FF[n]
                        if n == 0 and k < 3:
                            normed_in(k + 1)
                        act.wait_ge(gate_mm, i + 1)
                        if i >= 2:
                            act.wait_ge(u_done, i - 1)
                        nc.scalar.activation(gated[i % 2][0:width, :], PS[0:width, i % 2, :], ACT.Gelu, bias=ff_cols[0:width, 3 + n:4 + n]).then_inc(gelu_done, 1)

                @block.gpsimd
                def _(pool):
                    def split_weights(p):
                        pool.wait_ge(wqk_in, 16 * p + 16)
                        nc.gpsimd.tensor_tensor(w_parts[0][:, :].rearrange("p (i n) -> p i n", i=2), w_qk.rearrange("p (i n) -> p i n", i=2),
                                                ones[:, :].unsqueeze(1).broadcast_to([128, 2, 128]), ALU.mult).then_inc(w_split, 1)
                        pool.wait_ge(w_split, 2 * p + 1)
                        nc.gpsimd.tensor_tensor(w_parts[1][:, :], w_qk, w_parts[0][:, :], ALU.subtract).then_inc(w_split, 1)

                    def diagonal(r, g):
                        pool.wait_ge(mx_red, r * CHUNKS + (g + 1))
                        if g >= 3:
                            pool.wait_ge(st_full, r * CHUNKS + (g - 2))
                        nc.gpsimd.tensor_tensor(diag[g % 3][0:QC, :].rearrange("p (u n) -> p u n", u=4), ident[0:QC, 0:QC].unsqueeze(1).broadcast_to([QC, 4, QC]),
                                                neg_max[g % 4][0:QC, :].unsqueeze(2).broadcast_to([QC, 4, QC]), ALU.mult).then_inc(d_ready, 1)

                    def body(p, a, bb):
                        if isinstance(p, int) and a:
                            pool.wait_ge(tables, 2)
                        if a and not isinstance(p, int):
                            split_weights(p)
                        for s in range(STEPS):
                            if bb and s < CHUNKS:
                                diagonal(p - 1, s)
                            if a and s % 3 == 2 and s // 3 < 4:
                                i, quarter = s // 3, QUARTERS[s // 3]
                                pool.wait_ge(sq_done, 4 * p + (i + 1))
                                pool.wait_ge(add_done, 4 * p + i)
                                src = raw[:, 4 * quarter:4 * quarter + 4, :].rearrange("p t (w h d) -> p (t w) h d", w=2, h=2)
                                dst = cross.rearrange("p (c h d) -> p c h d", c=8, h=2)
                                tab = tab_b.rearrange("p (c d) -> p c d", d=64)[:, 8 * (quarter % 2):8 * (quarter % 2) + 8, :]
                                for o, other in ((0, 32), (32, 0)):
                                    nc.gpsimd.tensor_tensor(dst[:, :, :, o:o + 32], src[:, :, :, other:other + 32],
                                                                   tab[:, :, o:o + 32].unsqueeze(2).broadcast_to([128, 8, 2, 32]), ALU.mult).then_inc(t2_done, 1)

                    split_weights(0)
                    pool.wait_ge(scales_in, 8 * 16)
                    nc.gpsimd.tensor_tensor(tab_b.rearrange("p (t n) -> p t n", t=BT), base_b.rearrange("p (t n) -> p t n", t=BT),
                                            swapped.unsqueeze(1).broadcast_to([128, BT, 128]), ALU.mult).then_inc(tables, 1)
                    iterations(pool, body)

                    pool.wait_ge(ff_in, 6 * 16)
                    nc.gpsimd.tensor_copy(w1_parts[0][:, :], w1[:, :]).then_inc(w1_split, 1)
                    pool.wait_ge(w1_split, 1)
                    nc.gpsimd.tensor_tensor(w1_parts[1][:, :], w1[:, :], w1_parts[0][:, :], ALU.subtract).then_inc(w1_split, 1)
                    for k in range(4):
                        pool.wait_ge(xn_in, k + 1)
                        pool.wait_ge(xn_high, k + 1)
                        nc.gpsimd.tensor_tensor(x_parts[1][:, 512 * k:512 * k + 512], xnT[:, 512 * k:512 * k + 512], x_parts[0][:, 512 * k:512 * k + 512],
                                                ALU.subtract).then_inc(xn_low, 1)
                        for t in range(4 * k, 4 * k + 4):
                            nc.gpsimd.tensor_tensor(x_tok[:, t, :], x_tok[:, t, :], b2_row[:, :], ALU.add).then_inc(b2_added, 1)

                @block.vector
                def _(dve):
                    def maximum(r, g):
                        dve.wait_ge(mx_full, r * CHUNKS + (g + 1))
                        if g >= 4:
                            dve.wait_ge(d_ready, r * CHUNKS + (g - 3))
                        nc.vector.memset(gate[0:1, g % 2:g % 2 + 1], 0.0)
                        for u in range(4):
                            row = PS[0:QC, 2 + g % 2, 128 * u:128 * u + 128]
                            last = nc.vector.tensor_tensor_reduce(out=row, in0=row, in1=band_qk[g == 0][:, :], scale=-1.0, scalar=3.0e38,
                                                                  op0=ALU.add, op1=ALU.min, accum_out=neg_max[g % 4][0:QC, u:u + 1])
                        last.then_inc(mx_red, 1)

                    def outputs(r, g):
                        dve.wait_ge(den_done, r * CHUNKS + (g + 1))
                        nc.vector.tensor_tensor(oT[:, :, QC * g:QC * g + QC], PS[:, 6 + g % 2, 0:2 * QC].rearrange("p (b n) -> p b n", b=B),
                                                rec_den[g % 2].rearrange("p (b n) -> p b n", b=B), ALU.mult).then_inc(o_done, 1)

                    def late(p, s, a, bb):
                        for name in LATE.get(s, ()):
                            f, bank_free = int(name[1]), free[bank_of(name)]
                            if name[0] == "T" and a:
                                b, lo = QUARTERS[f // 2] // 2, 512 * (QUARTERS[f // 2] % 2)
                                dve.wait_ge(bank_free, before(p, name) + 1)
                                if f % 2:
                                    nc.vector.tensor_copy(qz_b[0:64, 0, b, lo:lo + 512], qz[0:64, 0, b, lo:lo + 512])
                                    nc.vector.tensor_copy(qz_b[64:128, 1, b, lo:lo + 512], qz[64:128, 1, b, lo:lo + 512]).then_inc(cast_done, 1)
                                else:
                                    nc.vector.tensor_copy(kT_b[:, b, PAD + lo:PAD + lo + 512], kT[:, b, PAD + lo:PAD + lo + 512]).then_inc(cast_done, 1)
                            if name[0] == "Y" and bb:
                                dve.wait_ge(full, fill(p, name) + 1)
                                xs = x_tok[:, 4 * f:4 * f + 4, :].rearrange("p t c -> p (t c)")
                                nc.vector.tensor_tensor(xs, PS[:, bank_of(name), :], xs, ALU.add).then_inc(bank_free, 1)

                    def body(p, a, bb):
                        r = p - 1
                        for s in range(STEPS):
                            if bb and s < CHUNKS:
                                maximum(r, s)
                            if bb and 0 <= s - 4 < CHUNKS:
                                outputs(r, s - 4)
                            if not a:
                                continue
                            if s % 3 == 2 and s // 3 < 4:
                                i, quarter = s // 3, QUARTERS[s // 3]
                                src = raw[:, 4 * quarter:4 * quarter + 4, :].rearrange("p t (w h d) -> p (t w) h d", w=2, h=2)
                                dst = rot[:, 4 * quarter:4 * quarter + 4, :].rearrange("p t (w h d) -> p (t w) h d", w=2, h=2)
                                tab = tab_a.rearrange("p (c d) -> p c d", d=64)[:, 8 * (quarter % 2):8 * (quarter % 2) + 8, :]
                                dve.wait_ge(sq_done, 4 * p + (i + 1))
                                dve.wait_ge(rn_ready, 4 * p + i)
                                nc.vector.tensor_reduce(norms2, squares.rearrange("p (c d) -> p c d", d=64), AX.X, ALU.add).then_inc(red_done, 1)
                                if i == 0 and not isinstance(p, int):
                                    dve.wait_ge(full, FILLS * p - 4)
                                nc.vector.tensor_tensor(dst, src, tab.unsqueeze(2).broadcast_to([128, 8, 2, 64]), ALU.mult).then_inc(t1_done, 1)
                                dve.wait_ge(red_done, 4 * p + (i + 1))
                                nc.vector.tensor_scalar(norms2, norms2, 1e-24, None, ALU.max).then_inc(n2_ready, 1)
                            if s % 3 == 0 and 1 <= s // 3 <= 4:
                                i, quarter = s // 3 - 1, QUARTERS[s // 3 - 1]
                                d = rot[:, 4 * quarter:4 * quarter + 4, :].rearrange("p t n -> p (t n)")
                                dve.wait_ge(t1_done, 4 * p + (i + 1))
                                dve.wait_ge(t2_done, 8 * p + (2 * i + 2))
                                nc.vector.tensor_tensor(d, d, cross, ALU.add).then_inc(add_done, 1)
                            if s % 3 == 1 and 1 <= s // 3 <= 4:
                                i, quarter = s // 3 - 1, QUARTERS[s // 3 - 1]
                                d = rot[:, 4 * quarter:4 * quarter + 4, :].rearrange("p t (c d) -> p (t c) d", d=64)
                                dve.wait_ge(add_done, 4 * p + (i + 1))
                                dve.wait_ge(rn_ready, 4 * p + (i + 1))
                                nc.vector.tensor_tensor(d, d, inv_norm.unsqueeze(2).broadcast_to([128, 16, 64]), ALU.mult).then_inc(rot_done, 1)
                            late(p, s - 1, a, bb)
                        late(p, STEPS - 1, a, bb)
                        late(p, STEPS, a, bb)

                    def split_x(n):
                        b, lo = QUARTERS[n] // 2, 512 * (QUARTERS[n] % 2)
                        high, low = (x[:, 512 * QUARTERS[n]:512 * QUARTERS[n] + 512] for x in x_parts)
                        dve.wait_ge(xt_in, n + 1)
                        nc.vector.tensor_copy(high, XT[:, b, PAD + lo:PAD + lo + 512]).then_inc(x_split, 1)
                        dve.wait_ge(x_split, 2 * n + 1)
                        nc.vector.tensor_tensor(low, XT[:, b, PAD + lo:PAD + lo + 512], high, ALU.subtract).then_inc(x_split, 1)

                    for n in range(4):
                        split_x(n)
                        if n == 1:
                            dve.wait_ge(scales_in, 8 * 16)
                            nc.vector.tensor_tensor(tab_a.rearrange("p (t n) -> p t n", t=BT), base_a.rearrange("p (t n) -> p t n", t=BT),
                                                    scales.unsqueeze(1).broadcast_to([128, BT, 128]), ALU.mult).then_inc(tables, 1)
                    dve.wait_ge(tables, 2)
                    iterations(dve, body)

                    dve.wait_ge(ff_in, 6 * 16)
                    def moments_of(k):
                        for t in range(4 * k, 4 * k + 4):
                            dve.wait_ge(back, 4 * k + 4)
                            nc.vector.bn_stats(stats[:, t, :], PS[:, 4 + k, 128 * (t % 4):128 * (t % 4) + 128]).then_inc(stat, 1)
                        for t in range(4 * k, 4 * k + 4):
                            dve.wait_ge(stat, 8 * k + t % 4 + 1)
                            nc.vector.bn_aggr(moments[:, t, :], stats[:, t, :]).then_inc(stat, 1)

                    def normalise(k):
                        for t in range(4 * k, 4 * k + 4):
                            dve.wait_ge(rs, k + 1)
                            nc.vector.tensor_scalar(xn_tok[:, t, :], PS[:, 4 + k, 128 * (t % 4):128 * (t % 4) + 128], moments[:, t, 0:1], rstd[:, t:t + 1],
                                                    ALU.subtract, ALU.mult).then_inc(normed, 1)

                    moments_of(0)
                    for k in range(1, 4):
                        moments_of(k)
                        normalise(k - 1)
                    normalise(3)

                    def y(k):
                        dve.wait_ge(y_mm, k + 1)
                        dve.wait_ge(b2_added, 4 * k + 4)
                        xs = x_tok[:, 4 * k:4 * k + 4, :].rearrange("p t c -> p (t c)")
                        nc.vector.tensor_tensor(xs, PS[:, 4 + k, :], xs, ALU.add)

                    for i, (k, n) in enumerate(items):
                        lo, width = FF[n]
                        dve.wait_ge(gelu_done, i + 1)
                        dve.wait_ge(a_mm, i + 1)
                        nc.vector.scalar_tensor_tensor(uT[n][0:width, 512 * k:512 * k + 512], PS[0:width, 2 + i % 2, :], ff_cols[0:width, n:n + 1],
                                                       gated[i % 2][0:width, :], ALU.add, ALU.mult).then_inc(u_done, 1)
                        if n == 2 and k:
                            y(k - 1)
                    y(3)

        with stage("none") as (block, none):
            @block.vector
            def _(dve):
                nc.vector.tensor_tensor(x_tok[:, :, :], x_tok[:, :, :], x_keep[:, :, :], ALU.add)

    setup()
    full_attention("lora")
    channel_mix()
    full_attention("causal")
    channel_mix()
    rg_lru()
    window_layers()
    full_attention("plain")
    window_layers()
    with stage("stored") as (block, stored):
        @block.sync
        def _(sp):
            sp.dma_start(out.rearrange("b (t p) c -> p (b t) c", p=128), x_tok[:, :, :]).then_inc(stored, 16)
            sp.wait_ge(stored, 16)
    ctx.close()


_INS = ["L0_attn_a_x", "L0_attn_a_W_qkv", "L0_attn_a_b_qkv", "L0_attn_a_B_qkv", "L0_attn_a_W_proj", "L0_attn_a_b_proj",
        "L0_attn_a_B_proj", "L0_attn_b_b_attn", "L0_attn_b_b_proj", "L0_ffn_mu_r", "L0_ffn_mu_k",
        "L1_attn_a_conv_b", "L1_attn_a_rg_in_b", "L1_attn_a_rg_gate_b", "L1_attn_a_forget_lambda", "L1_attn_a_norm1_w", "L1_attn_a_norm2_w",
        "L1_attn_b_bq", "L1_attn_b_bk", "L1_attn_b_bv", "L1_attn_b_bo",
        "L1_ffn_q_scale", "L1_ffn_k_scale", "L1_ffn_W1", "L1_ffn_W2", "L1_ffn_b2"]
_TRANSPOSED = {"t_A_qkv": "L0_attn_a_A_qkv", "t_A_proj": "L0_attn_a_A_proj", "t_w_attn": "L0_attn_b_w_attn", "t_w_proj": "L0_attn_b_w_proj",
               "t_W_r": "L0_ffn_W_r", "t_W_k": "L0_ffn_W_k", "t_W_v": "L0_ffn_W_v",
               "t_W_in": "L1_attn_a_W_in", "t_W_gate": "L1_attn_a_W_gate", "t_W_out": "L1_attn_a_W_out",
               "t_rg_in": "L1_attn_a_rg_in_w", "t_rg_gate": "L1_attn_a_rg_gate_w",
               "t_mlp_gate": "L1_attn_a_mlp_gate_w", "t_mlp_up": "L1_attn_a_mlp_up_w", "t_mlp_down": "L1_attn_a_mlp_down_w",
               "t_Wq": "L1_attn_b_Wq", "t_Wk": "L1_attn_b_Wk", "t_Wv": "L1_attn_b_Wv", "t_Wo": "L1_attn_b_Wo"}


def laid_out(inputs):
    arrays = {name: np.ascontiguousarray(inputs[name]) for name in _INS}
    for name, of in _TRANSPOSED.items():
        arrays[name] = np.ascontiguousarray(np.asarray(inputs[of]).T)
    arrays["conv_w"] = np.ascontiguousarray(np.asarray(inputs["L1_attn_a_conv_w"])[:, 0, :])
    def dimension_first(a):
        parts = a.reshape(*a.shape[:-1], -1, 4, HD)
        return np.ascontiguousarray(np.swapaxes(parts, -1, -2)).reshape(a.shape)

    for name in ("L0_attn_a_W_qkv", "L0_attn_a_B_qkv", "L0_attn_a_b_qkv", "t_w_attn", "L0_attn_b_b_attn"):
        a = arrays[name]
        arrays[name] = np.concatenate([dimension_first(a[..., :2 * C]), a[..., 2 * C:]], axis=-1)
    for name in ("t_Wq", "t_Wk", "L1_attn_b_bq", "L1_attn_b_bk"):
        arrays[name] = dimension_first(arrays[name])
    w = np.asarray(inputs["L1_ffn_Wqkv"]).reshape(DEPTH, C, 3, PAIRS, 128)
    arrays["w_pairs"] = np.ascontiguousarray(w.transpose(0, 3, 1, 2, 4).reshape(DEPTH * PAIRS, C, 384))
    arrays["w_out_pairs"] = np.ascontiguousarray(np.asarray(inputs["L1_ffn_Wo"]).reshape(DEPTH * PAIRS, 128, C))
    chunks = [(0, 128), (128, 128), (256, INNER - 256)]
    cols = np.zeros((DEPTH, 128, 8), np.float32)
    b1 = np.asarray(inputs["L1_ffn_b1"])
    for n, (lo, width) in enumerate(chunks):
        cols[:, :width, n] = b1[:, lo:lo + width]
        cols[:, :width, 3 + n] = b1[:, INNER + lo:INNER + lo + width]
    cols[:, :, 6] = inputs["L1_ffn_ln_g"]
    cols[:, :, 7] = inputs["L1_ffn_ln_b"]
    arrays["ff_cols"] = cols
    arrays.update(shape_constants())
    return arrays


def kernel(**inputs):
    import concourse.bacc as bacc
    from concourse.bass_utils import run_bass_kernel_spmd

    nc = bacc.Bacc("TRN2", target_bir_lowering=False, num_devices=1)
    arrays = laid_out(inputs)
    I = {name: nc.dram_tensor("in_" + name, a.shape, mybir.dt.from_np(a.dtype), kind="ExternalInput").ap() for name, a in arrays.items()}
    out = nc.dram_tensor("out", (B, N, C), F32, kind="ExternalOutput").ap()
    build(nc, I, out)
    results = run_bass_kernel_spmd(nc, [{"in_" + name: a for name, a in arrays.items()}], core_ids=[0]).results
    return results[0]["out"]
```
